# Optimizing a Trainium2 kernel written in Bass

```python
import numpy as np
import jax
import jax.numpy as jnp

def _softmax(x, axis=-1):
    return jax.nn.softmax(x, axis=axis)

def _gelu(x):
    return jax.nn.gelu(x, approximate=True)

def _silu(x):
    return jax.nn.silu(x)

def _sigmoid(x):
    return jax.nn.sigmoid(x)

def _layernorm(x, axis=-1, eps=1e-05):
    m = jnp.mean(x, axis=axis, keepdims=True)
    v = jnp.var(x, axis=axis, keepdims=True)
    return (x - m) / jnp.sqrt(v + eps)

def _scatter_add(tgt, idx, src, axis=0):
    return tgt.at[idx].add(src)

def _segment_sum(src, seg, n):
    return jax.ops.segment_sum(src, seg, n)
kernel_name = 'mk_early_fusion_d1_tok_img768_r4_040168'

def setup_inputs(seed: int=0):
    np.random.seed(seed)
    _w = jnp.asarray

    def _rec_inputs():
        import jax
        import jax.numpy as jnp
        _rk = jax.random.key(seed)
        x = -0.000222058 + 0.999998 * jax.random.normal(jax.random.fold_in(_rk, 1), (32, 3, 128, 128), jnp.float32)
        txt = 0.000626447 + 0.554253 * jax.random.normal(jax.random.fold_in(_rk, 2), (32, 77, 192), jnp.float32)
        return (x, txt)
    x, txt = _rec_inputs()

    def _L0_tok_setup():
        import jax, jax.numpy as jnp
        import numpy as np
        from jax import lax
        HIDDEN = 192
        C_IN = 3
        PATCH = 16
        SIDE = 32
        NUM_PATCHES = SIDE * SIDE

        def _position_ids(nb_h, nb_w):
            boundaries = np.arange(1.0 / SIDE, 1.0, 1.0 / SIDE, dtype=np.float32)
            frac_h = np.arange(0.0, 1.0 - 1e-06, 1.0 / nb_h, dtype=np.float32)
            frac_w = np.arange(0.0, 1.0 - 1e-06, 1.0 / nb_w, dtype=np.float32)
            bh = np.searchsorted(boundaries, frac_h, side='right')
            bw = np.searchsorted(boundaries, frac_w, side='right')
            return jnp.asarray((bh[:, None] * SIDE + bw).reshape(-1), dtype=jnp.int32)
        key = jax.random.key(seed)
        k1, k2, k3 = jax.random.split(key, 3)
        pixel_values = jax.random.normal(k1, (32, C_IN, 128, 128), dtype=jnp.float32)
        conv_w = jax.random.normal(k2, (HIDDEN, C_IN, PATCH, PATCH), dtype=jnp.float32) * 0.02
        conv_b = jnp.zeros((HIDDEN,), dtype=jnp.float32)
        pos_table = jax.random.normal(k3, (NUM_PATCHES, HIDDEN), dtype=jnp.float32) * 0.02
        return {'pixel_values': pixel_values, 'conv_w': conv_w, 'conv_b': conv_b, 'pos_table': pos_table}
    _L0_tok_all = _L0_tok_setup()
    _L0_tok_in = {k: v for k, v in _L0_tok_all.items() if k in ('conv_w', 'conv_b', 'pos_table')}
    del _L0_tok_all

    def _L0_attn_setup():
        import jax, jax.numpy as jnp
        import numpy as np
        D_MODEL = 192
        D_INNER = 384
        D_STATE = 16
        DT_RANK = 96
        H_FFN = 512
        B, L = (1, 512)
        EPS = 1e-06

        def rmsnorm(x, w):
            return x * jax.lax.rsqrt(jnp.mean(x * x, axis=-1, keepdims=True) + EPS) * w

        def selective_scan(z, W_xproj, W_dt, b_dt, A_log, D_skip):
            xdbl = jnp.einsum('bld,kd->blk', z, W_xproj)
            dt_in, Bm, Cm = jnp.split(xdbl, [DT_RANK, DT_RANK + D_STATE], axis=-1)
            dt = jax.nn.softplus(jnp.einsum('blr,dr->bld', dt_in, W_dt) + b_dt)
            A = -jnp.exp(A_log)
            A_bar = jnp.exp(dt[..., None] * A)
            Bx = (dt * z)[..., None] * Bm[:, :, None, :]

            def comb(e1, e2):
                a1, b1 = e1
                a2, b2 = e2
                return (a1 * a2, a2 * b1 + b2)
            _, h = jax.lax.associative_scan(comb, (A_bar, Bx), axis=1)
            y = jnp.einsum('blds,bls->bld', h, Cm) + D_skip * z
            return y
        key = jax.random.key(seed)
        ks = jax.random.split(key, 10)
        s = lambda k, shape, scale=0.02: jax.random.normal(k, shape, dtype=jnp.float32) * scale
        return {'x': jax.random.normal(ks[0], (B, L, D_MODEL), dtype=jnp.float32), 'w_norm1': jnp.ones((D_MODEL,), jnp.float32), 'W_in': s(ks[1], (D_INNER, D_MODEL)), 'W_gate': s(ks[2], (D_INNER, D_MODEL)), 'W_xproj': s(ks[3], (DT_RANK + 2 * D_STATE, D_INNER)), 'W_dt': s(ks[4], (D_INNER, DT_RANK)), 'b_dt': jnp.full((D_INNER,), -4.6, jnp.float32), 'A_log': jnp.log(jnp.tile(jnp.arange(1, D_STATE + 1, dtype=jnp.float32), (D_INNER, 1))), 'D_skip': jnp.ones((D_INNER,), jnp.float32), 'W_out': s(ks[5], (D_MODEL, D_INNER)), 'w_ffn_norm': jnp.ones((D_MODEL,), jnp.float32), 'W_up': s(ks[6], (H_FFN, D_MODEL)), 'W_gate_ffn': s(ks[7], (H_FFN, D_MODEL)), 'W_down': s(ks[8], (D_MODEL, H_FFN))}
    _L0_attn_all = _L0_attn_setup()
    _L0_attn_in = {k: v for k, v in _L0_attn_all.items() if k in ('w_norm1', 'W_in', 'W_gate', 'W_xproj', 'W_dt', 'b_dt', 'A_log', 'D_skip', 'W_out', 'w_ffn_norm', 'W_up', 'W_gate_ffn', 'W_down')}
    del _L0_attn_all

    def _L0_ffn_setup():
        import jax, jax.numpy as jnp
        import numpy as np
        E = 192
        H = 12
        D = E // H
        HID = 768
        NEXP = 4
        TOPK = 2
        EPS = 1e-05

        def _ln(x, g, b):
            m = jnp.mean(x, axis=-1, keepdims=True)
            v = jnp.mean(jnp.square(x - m), axis=-1, keepdims=True)
            return (x - m) * jax.lax.rsqrt(v + EPS) * g + b
        key = jax.random.key(seed)
        ks = jax.random.split(key, 10)
        s = 0.02
        return {'x': jax.random.normal(ks[0], (8, 256, E), jnp.float32), 'ln1_g': jnp.ones((E,), jnp.float32), 'ln1_b': jnp.zeros((E,), jnp.float32), 'in_w': jax.random.normal(ks[1], (3 * E, E), jnp.float32) * s, 'in_b': jnp.zeros((3 * E,), jnp.float32), 'out_w': jax.random.normal(ks[2], (E, E), jnp.float32) * s, 'out_b': jnp.zeros((E,), jnp.float32), 'mlp_w1': jax.random.normal(ks[3], (E, HID), jnp.float32) * s, 'mlp_b1': jnp.zeros((HID,), jnp.float32), 'mlp_w2': jax.random.normal(ks[4], (HID, E), jnp.float32) * s, 'mlp_b2': jnp.zeros((E,), jnp.float32), 'ln2_g': jnp.ones((E,), jnp.float32), 'ln2_b': jnp.zeros((E,), jnp.float32), 'gate_w': jax.random.normal(ks[5], (NEXP, E), jnp.float32) * s, 'gate_b': jnp.zeros((NEXP,), jnp.float32), 'exp_w1': jax.random.normal(ks[6], (NEXP, E, HID), jnp.float32) * s, 'exp_b1': jnp.zeros((NEXP, HID), jnp.float32), 'exp_w2': jax.random.normal(ks[7], (NEXP, HID, E), jnp.float32) * s, 'exp_b2': jnp.zeros((NEXP, E), jnp.float32)}
    _L0_ffn_all = _L0_ffn_setup()
    _L0_ffn_in = {k: v for k, v in _L0_ffn_all.items() if k in ('ln1_g', 'ln1_b', 'in_w', 'in_b', 'out_w', 'out_b', 'mlp_w1', 'mlp_b1', 'mlp_w2', 'mlp_b2', 'ln2_g', 'ln2_b', 'gate_w', 'gate_b', 'exp_w1', 'exp_b1', 'exp_w2', 'exp_b2')}
    del _L0_ffn_all
    return {'x': x, 'txt': txt, 'L0_tok_conv_w': _L0_tok_in['conv_w'], 'L0_tok_conv_b': _L0_tok_in['conv_b'], 'L0_tok_pos_table': _L0_tok_in['pos_table'], 'L0_attn_w_norm1': _L0_attn_in['w_norm1'], 'L0_attn_W_in': _L0_attn_in['W_in'], 'L0_attn_W_gate': _L0_attn_in['W_gate'], 'L0_attn_W_xproj': _L0_attn_in['W_xproj'], 'L0_attn_W_dt': _L0_attn_in['W_dt'], 'L0_attn_b_dt': _L0_attn_in['b_dt'], 'L0_attn_A_log': _L0_attn_in['A_log'], 'L0_attn_D_skip': _L0_attn_in['D_skip'], 'L0_attn_W_out': _L0_attn_in['W_out'], 'L0_attn_w_ffn_norm': _L0_attn_in['w_ffn_norm'], 'L0_attn_W_up': _L0_attn_in['W_up'], 'L0_attn_W_gate_ffn': _L0_attn_in['W_gate_ffn'], 'L0_attn_W_down': _L0_attn_in['W_down'], 'L0_ffn_ln1_g': _L0_ffn_in['ln1_g'], 'L0_ffn_ln1_b': _L0_ffn_in['ln1_b'], 'L0_ffn_in_w': _L0_ffn_in['in_w'], 'L0_ffn_in_b': _L0_ffn_in['in_b'], 'L0_ffn_out_w': _L0_ffn_in['out_w'], 'L0_ffn_out_b': _L0_ffn_in['out_b'], 'L0_ffn_mlp_w1': _L0_ffn_in['mlp_w1'], 'L0_ffn_mlp_b1': _L0_ffn_in['mlp_b1'], 'L0_ffn_mlp_w2': _L0_ffn_in['mlp_w2'], 'L0_ffn_mlp_b2': _L0_ffn_in['mlp_b2'], 'L0_ffn_ln2_g': _L0_ffn_in['ln2_g'], 'L0_ffn_ln2_b': _L0_ffn_in['ln2_b'], 'L0_ffn_gate_w': _L0_ffn_in['gate_w'], 'L0_ffn_gate_b': _L0_ffn_in['gate_b'], 'L0_ffn_exp_w1': _L0_ffn_in['exp_w1'], 'L0_ffn_exp_b1': _L0_ffn_in['exp_b1'], 'L0_ffn_exp_w2': _L0_ffn_in['exp_w2'], 'L0_ffn_exp_b2': _L0_ffn_in['exp_b2']}

def reference(x, txt, L0_tok_conv_w, L0_tok_conv_b, L0_tok_pos_table, L0_attn_w_norm1, L0_attn_W_in, L0_attn_W_gate, L0_attn_W_xproj, L0_attn_W_dt, L0_attn_b_dt, L0_attn_A_log, L0_attn_D_skip, L0_attn_W_out, L0_attn_w_ffn_norm, L0_attn_W_up, L0_attn_W_gate_ffn, L0_attn_W_down, L0_ffn_ln1_g, L0_ffn_ln1_b, L0_ffn_in_w, L0_ffn_in_b, L0_ffn_out_w, L0_ffn_out_b, L0_ffn_mlp_w1, L0_ffn_mlp_b1, L0_ffn_mlp_w2, L0_ffn_mlp_b2, L0_ffn_ln2_g, L0_ffn_ln2_b, L0_ffn_gate_w, L0_ffn_gate_b, L0_ffn_exp_w1, L0_ffn_exp_b1, L0_ffn_exp_w2, L0_ffn_exp_b2):
    import jax
    import jax.numpy as jnp

    def _L0_tok_ref(pixel_values, conv_w, conv_b, pos_table):
        import jax, jax.numpy as jnp
        import numpy as np
        from jax import lax
        HIDDEN = 192
        C_IN = 3
        PATCH = 16
        SIDE = 32
        NUM_PATCHES = SIDE * SIDE

        def _position_ids(nb_h, nb_w):
            boundaries = np.arange(1.0 / SIDE, 1.0, 1.0 / SIDE, dtype=np.float32)
            frac_h = np.arange(0.0, 1.0 - 1e-06, 1.0 / nb_h, dtype=np.float32)
            frac_w = np.arange(0.0, 1.0 - 1e-06, 1.0 / nb_w, dtype=np.float32)
            bh = np.searchsorted(boundaries, frac_h, side='right')
            bw = np.searchsorted(boundaries, frac_w, side='right')
            return jnp.asarray((bh[:, None] * SIDE + bw).reshape(-1), dtype=jnp.int32)
        B, _, H, W = pixel_values.shape
        nb_h, nb_w = (H // PATCH, W // PATCH)
        patches = lax.conv_general_dilated(pixel_values, conv_w, window_strides=(PATCH, PATCH), padding='VALID', dimension_numbers=('NCHW', 'OIHW', 'NCHW'))
        patches = patches + conv_b[None, :, None, None]
        embeddings = patches.reshape(B, HIDDEN, nb_h * nb_w).transpose(0, 2, 1)
        pos_ids = _position_ids(nb_h, nb_w)
        pos_emb = pos_table[pos_ids]
        return embeddings + pos_emb[None, :, :]

    def _L0_attn_ref(x, w_norm1, W_in, W_gate, W_xproj, W_dt, b_dt, A_log, D_skip, W_out, w_ffn_norm, W_up, W_gate_ffn, W_down):
        import jax, jax.numpy as jnp
        import numpy as np
        D_MODEL = 192
        D_INNER = 384
        D_STATE = 16
        DT_RANK = 96
        H_FFN = 512
        B, L = (1, 512)
        EPS = 1e-06

        def rmsnorm(x, w):
            return x * jax.lax.rsqrt(jnp.mean(x * x, axis=-1, keepdims=True) + EPS) * w

        def selective_scan(z, W_xproj, W_dt, b_dt, A_log, D_skip):
            xdbl = jnp.einsum('bld,kd->blk', z, W_xproj)
            dt_in, Bm, Cm = jnp.split(xdbl, [DT_RANK, DT_RANK + D_STATE], axis=-1)
            dt = jax.nn.softplus(jnp.einsum('blr,dr->bld', dt_in, W_dt) + b_dt)
            A = -jnp.exp(A_log)
            A_bar = jnp.exp(dt[..., None] * A)
            Bx = (dt * z)[..., None] * Bm[:, :, None, :]

            def comb(e1, e2):
                a1, b1 = e1
                a2, b2 = e2
                return (a1 * a2, a2 * b1 + b2)
            _, h = jax.lax.associative_scan(comb, (A_bar, Bx), axis=1)
            y = jnp.einsum('blds,bls->bld', h, Cm) + D_skip * z
            return y
        residual = x
        h = rmsnorm(x, w_norm1)
        z = h @ W_in.T
        z = z * jax.nn.sigmoid(h @ W_gate.T)
        y = selective_scan(z, W_xproj, W_dt, b_dt, A_log, D_skip)
        x = residual + y @ W_out.T
        hf = rmsnorm(x, w_ffn_norm)
        ffn = jax.nn.silu(hf @ W_gate_ffn.T) * (hf @ W_up.T) @ W_down.T
        return x + ffn

    def _L0_ffn_ref(x, ln1_g, ln1_b, in_w, in_b, out_w, out_b, mlp_w1, mlp_b1, mlp_w2, mlp_b2, ln2_g, ln2_b, gate_w, gate_b, exp_w1, exp_b1, exp_w2, exp_b2):
        import jax, jax.numpy as jnp
        import numpy as np
        E = 192
        H = 12
        D = E // H
        HID = 768
        NEXP = 4
        TOPK = 2
        EPS = 1e-05

        def _ln(x, g, b):
            m = jnp.mean(x, axis=-1, keepdims=True)
            v = jnp.mean(jnp.square(x - m), axis=-1, keepdims=True)
            return (x - m) * jax.lax.rsqrt(v + EPS) * g + b
        B, N, _ = x.shape
        h = _ln(x, ln1_g, ln1_b)
        qkv = h @ in_w.T + in_b
        q, k, v = jnp.split(qkv, 3, axis=-1)
        q = q.reshape(B, N, H, D)
        k = k.reshape(B, N, H, D)
        v = v.reshape(B, N, H, D)
        scores = jnp.einsum('bqhd,bkhd->bhqk', q, k) / jnp.sqrt(jnp.float32(D))
        attn = jax.nn.softmax(scores, axis=-1)
        ctx = jnp.einsum('bhqk,bkhd->bqhd', attn, v).reshape(B, N, E)
        x = x + ctx @ out_w.T + out_b
        x = x + jax.nn.gelu(x @ mlp_w1 + mlp_b1, approximate=False) @ mlp_w2 + mlp_b2
        xm = _ln(x, ln2_g, ln2_b)
        logits = xm @ gate_w.T + gate_b
        topv, topi = jax.lax.top_k(logits, TOPK)
        gates = jax.nn.softmax(topv, axis=-1)
        onehot = jax.nn.one_hot(topi, NEXP, dtype=x.dtype)
        comb = jnp.einsum('bnk,bnke->bne', gates, onehot)
        moe_out = jnp.zeros_like(x)
        for e in range(NEXP):
            he = jax.nn.gelu(xm @ exp_w1[e] + exp_b1[e], approximate=False)
            oe = he @ exp_w2[e] + exp_b2[e]
            moe_out = moe_out + comb[..., e:e + 1] * oe
        return x + moe_out
    h = _L0_tok_ref(x, L0_tok_conv_w, L0_tok_conv_b, L0_tok_pos_table)
    h = jnp.concatenate([h, txt], axis=1)
    h = h + _L0_attn_ref(_layernorm(h, axis=-1), L0_attn_w_norm1, L0_attn_W_in, L0_attn_W_gate, L0_attn_W_xproj, L0_attn_W_dt, L0_attn_b_dt, L0_attn_A_log, L0_attn_D_skip, L0_attn_W_out, L0_attn_w_ffn_norm, L0_attn_W_up, L0_attn_W_gate_ffn, L0_attn_W_down)
    h = h + _L0_ffn_ref(_layernorm(h, axis=-1), L0_ffn_ln1_g, L0_ffn_ln1_b, L0_ffn_in_w, L0_ffn_in_b, L0_ffn_out_w, L0_ffn_out_b, L0_ffn_mlp_w1, L0_ffn_mlp_b1, L0_ffn_mlp_w2, L0_ffn_mlp_b2, L0_ffn_ln2_g, L0_ffn_ln2_b, L0_ffn_gate_w, L0_ffn_gate_b, L0_ffn_exp_w1, L0_ffn_exp_b1, L0_ffn_exp_w2, L0_ffn_exp_b2)
    return h

_drawn_inputs = setup_inputs


def setup_inputs(seed=0):
    import zlib

    import numpy as np

    out = dict(_drawn_inputs(seed))
    spreads = {'L0_tok_conv_b': (0.0, 0.1),
     'L0_attn_w_norm1': (1.0, 0.6),
     'L0_attn_b_dt': (-4.599999904632568, 0.6),
     'L0_attn_D_skip': (1.0, 0.6),
     'L0_attn_w_ffn_norm': (1.0, 0.6),
     'L0_ffn_ln1_g': (1.0, 0.6),
     'L0_ffn_ln1_b': (0.0, 0.8),
     'L0_ffn_in_b': (0.0, 0.716),
     'L0_ffn_out_b': (0.0, 0.636),
     'L0_ffn_mlp_b1': (0.0, 1.534),
     'L0_ffn_mlp_b2': (0.0, 0.567),
     'L0_ffn_ln2_g': (1.0, 0.6),
     'L0_ffn_ln2_b': (0.0, 2.0),
     'L0_ffn_gate_b': (0.0, 1.325),
     'L0_ffn_exp_b1': (0.0, 2.0),
     'L0_ffn_exp_b2': (0.0, 0.87)}
    factors = {'L0_attn_W_gate': 8.0,
     'L0_attn_W_xproj': 8.0,
     'L0_attn_W_dt': 8.0,
     'L0_attn_A_log': 8.0,
     'L0_attn_W_up': 4.488,
     'L0_attn_W_gate_ffn': 4.528,
     'L0_attn_W_down': 4.503,
     'L0_ffn_in_w': 8.0,
     'L0_ffn_out_w': 4.351,
     'L0_ffn_gate_w': 3.44,
     'L0_ffn_exp_w1': 3.843}
    for name, (base, spread) in spreads.items():
        noise = np.random.default_rng([zlib.crc32(name.encode()), seed]).standard_normal(out[name].shape)
        drawn = base * np.exp(spread * noise) if base else spread * noise
        out[name] = jnp.asarray(drawn.astype(out[name].dtype))
    for name, factor in factors.items():
        out[name] = (out[name] * factor).astype(out[name].dtype)
    return out
```

```python
import concourse.bass as bass
from concourse import mybir
from contextlib import ExitStack

ALU = mybir.AluOpType
ACT = mybir.ActivationFunctionType
AX = mybir.AxisListType
F32 = mybir.dt.float32

B, C_IN, IMG, PATCH = 32, 3, 128, 16
SIDE = IMG // PATCH
NP, NTXT = SIDE * SIDE, 77
L = NP + NTXT
E = 192
E1 = E - 128
KC = C_IN * PATCH * PATCH // 128
GB = 4
G = B // GB
N = GB * L
CH = N // 2
TILES = [(t, min(128, N - t)) for t in range(0, N, 128)]
NT = len(TILES)
DI, S, R = 384, 16, 96
MD = DI // 128
HF = 512
MF = HF // 128
H, HD = 12, E // 12
HP = 32
MH = H * HP // 128
HID, NEXP = 768, 4
MM = HID // 128
LH = [(0, 71), (71, 70)]
VW = HD + 1
LP = L + 1
NPAD = GB * LP
STEPS = S * MD
BURST = 6
NB = STEPS // BURST
NABAR, NRING, NBC, NROW = 7, 4, 2, 4
SPC = 30.0

VEC = {}
for _name, _w in (("w1n", 2), ("wfn", 2), ("g1", 2), ("b1", 2), ("g2", 2), ("b2", 2), ("bdt", MD),
                  ("alog", MD * S), ("dsk", MD), ("qb", MH), ("kb", MH), ("mb1", MM), ("eb1", NEXP * MM)):
    VEC[_name] = (sum(w for _, w in VEC.values()), _w)
VW_ALL = sum(w for _, w in VEC.values())

WEIGHTS = {"cw": (KC, E), "win": (2, DI), "wgate": (2, DI), "wxp": (MD, 128), "wdt": (1, DI), "wout": (MD, E),
           "wgf": (2, HF), "wup": (2, HF), "wdn": (MF, E), "wq": (2, MH * 128), "wk": (2, MH * 128),
           "wv": (2, E), "wo": (2, E), "mw1": (2, HID), "mw2": (MM, E), "gw": (2, NEXP),
           "ew1": (NEXP * 2, HID), "ew2": (NEXP * MM, E)}
ORDER = ["cw", "win", "wgate", "wxp", "wdt", "wout", "wgf", "wup", "wdn", "wq", "wk", "wv", "wo",
         "mw1", "mw2", "gw", "ew1", "ew2"]


class Signal:

    def __init__(self, sem, per):
        self.sem, self.per = sem, per

    def at(self, g, k=None):
        return g * self.per + (self.per if k is None else k)


class Chain:

    def __init__(self, signal, eng):
        self.rises, self.eng, self.k, self.g = signal, eng, 0, 0

    def begin(self, g):
        self.g, self.k = g, 0

    def link(self, ins):
        self.k += 1
        ins.then_inc(self.rises.sem, 1)
        self.eng.wait_ge(self.rises.sem, self.rises.at(self.g, self.k))

    def end(self):
        assert self.k == self.rises.per, self.k


def early_fusion_program(nc, dram, out):
    with ExitStack() as ctx:
        def sb(name, *shape):
            return ctx.enter_context(nc.sbuf_tensor(name, list(shape), F32))

        def signal(name, per):
            return Signal(ctx.enter_context(nc.semaphore(name)), per)

        W = {n: sb("w_" + n, 128, *WEIGHTS[n]) for n in ORDER}
        vec = sb("vec", 128, VW_ALL)
        ident = sb("ident", 128, 128)
        posb = sb("posb", 128, E)
        mb2 = sb("mb2", 128, E)
        eb2 = sb("eb2", NEXP, E)
        earlier = sb("earlier", 128, NEXP, NEXP)
        negA = sb("negA", 128, MD * S)
        half = sb("half", 128, NT)
        h0 = sb("h0", 128, NT, E)
        xa = sb("xa", 128, NT, E)
        hn = sb("hn", 128, NT, E)
        acc2 = sb("acc2", 128, NT, E)
        hT = sb("hT", 128, 2, N)
        xmT = sb("xmT", 128, 2, N)
        ge = sb("ge", 128, MM, N)
        xp = sb("xp", 128, KC, GB * NP)
        cv = sb("cv", 128, 2, E)
        xd = sb("xd", 128, N)
        negm = sb("negm", 128, 2, MH * 128)
        stats = sb("stats", 128, NT, 6)
        mv = sb("mv", 128, NT, 2)
        sm = sb("sm", 128, 8, NT)
        gs = sb("gs", 128, 8, NT * NEXP)
        gr = sb("gr", 128, 2, NT, NEXP * NEXP)
        gm = sb("gm", 128, 3, NT)
        comb = sb("comb", 128, NT, NEXP)
        combT = sb("combT", NEXP, N)
        region = sb("region", 128, 3 * MD * N + NABAR * NPAD + NRING * NPAD + NBC * 2 * N)
        o = 0

        def cut(n, width):
            nonlocal o
            v = region[:, o:o + n * width].rearrange("p (a b) -> p a b", a=n)
            o += n * width
            return v

        zu = cut(MD, N)
        dt = cut(MD, N)
        acc = cut(MD, N)
        abar = cut(NABAR, NPAD)
        ring = cut(NRING, NPAD)
        bc = cut(NBC, 2 * N)
        o = 3 * MD * N
        gf = cut(MF, N)
        o = 0
        qT = cut(MH, N)
        kT = cut(MH, N)
        qa = cut(MH, N)
        pT = cut(2 * H, L)
        vaug = cut(2 * GB, H * VW)
        o = 0
        g1 = cut(MM, N)
        brows = sb("brows", 128, 2 * N)

        th = sb("th", 128, 2, CH)

        def tanh_of(u):
            return th[:, u % 2, :]

        def ctxr(q):
            return cv[:, q, :]

        P = ctx.enter_context(nc.psum_tensor("P", [128, 8, 512], F32))

        def V(name, i=0, rows=128):
            return vec[0:rows, VEC[name][0] + i:VEC[name][0] + i + 1]

        s_w = signal("weights_in", 0)
        s_c = signal("constants_in", 0)
        s_setup = signal("setup_done", 0)
        s_past = {n: signal("past_wait_" + n, 0) for n in ("pe", "dve", "pool")}
        s_negA = signal("negA_ready", 0)
        s_xp = signal("patches_in", 16)
        s_txt = signal("text_in", 16)
        s_place = signal("patches_placed", 64)
        s_row = [signal(f"rows_in_{r}", 32 * S // NROW) for r in range(NROW)]
        s_out = signal("out_written", 16 * NT)
        s_conv, e_conv = signal("conv_done", 2), signal("conv_evac", 2)
        s_norm = signal("normalised", 4 * NT)
        s_tr, e_tr = signal("transposed", 10), signal("transposed_evac", 20)
        s_mv, s_sc = signal("moments", 4), signal("scales", 4)
        s_zg, s_tanh, e_z = signal("z_gate_done", 6), signal("z_tanh", 6), signal("z_evac", 6)
        s_xpj, e_xpj = signal("xproj_done", 2), signal("xproj_evac", 2)
        s_dtp, s_dtc, s_sp, e_dt = signal("dt_done", 6), signal("dt_clamped", 6), signal("softplus_log", 6), signal("dt_evac", 6)
        s_acc0 = signal("acc_init", MD)
        s_rst = signal("scan_reset", 1)
        s_bc = signal("bc_broadcast", S)
        s_ab = signal("abar_ready", STEPS)
        s_bx, s_h, s_hc = signal("bx", STEPS), signal("h", STEPS), signal("hc", STEPS)
        s_add = signal("y_added", STEPS)
        s_wo, e_wo = signal("wout_done", NT), signal("wout_evac", NT)
        s_gu, s_tg, e_gu = signal("gate_up_done", 8), signal("ffn_tanh", 8), signal("gate_up_evac", 8)
        s_wd, e_wd = signal("down_done", NT), signal("down_evac", NT)
        s_qk, e_qk = signal("qk_done", 12), signal("qk_evac", 12)
        s_v, e_v = signal("v_done", 8), signal("v_evac", 8)
        s_S, e_S = signal("scores_done", 4 * GB), signal("maxima", 4 * GB)
        s_nm, e_nm = signal("maxT_done", GB), signal("maxT_added", GB)
        s_S2, e_S2 = signal("scoresT_done", 4 * GB), signal("exp_done", 4 * GB)
        s_cx, e_cx = signal("ctx_done", GB), signal("ctx_evac", 2 * GB)
        s_cT, e_cT = signal("ctxT_done", GB), signal("ctxT_evac", 2 * GB)
        s_ow, e_ow = signal("attn_out_done", NT), signal("attn_out_evac", NT)
        s_x5b = signal("x5_plus_bias", NT)
        s_m1, e_m1 = signal("mlp1_done", 12), signal("mlp1_evac", 12)
        s_m2, e_m2 = signal("mlp2_done", NT), signal("mlp2_evac", NT)
        s_h1x = signal("h1_plus_x6", NT)
        s_lg, e_lg = signal("logits_done", 1), signal("logits_evac", 1)
        s_mx, s_ex = signal("logits_shifted", 1), signal("gate_exp", 1)
        s_cmb, s_cbT, e_cbT = signal("comb_done", 1), signal("combT_done", 2), signal("combT_evac", 2)
        s_b2, e_b2 = signal("b2_done", NT), signal("b2_evac", NT)
        s_e1, e_e1 = signal("expert1_done", 48), signal("expert1_evac", 48)
        s_e2, e_e2 = signal("expert2_done", NEXP * NT), signal("expert2_evac", NEXP * NT)
        c_dve, c_pool, c_act = signal("dve_chain", 34), signal("pool_chain", 16), signal("act_chain", 6)

        SETUP = 13

        def hold(eng, name):
            eng.sem_inc(s_past[name].sem, 1)

        def padded(view):
            return view.rearrange("p (b l) -> p b l", b=GB)[:, :, 1:LP]

        def tok(view):
            return view.rearrange("p (b l) -> p b l", b=GB)

        block = ctx.enter_context(nc.Block())

        @block.sync
        def _(sp):
            for n in ORDER:
                sp.dma_start(W[n][:], dram[n]).then_inc(s_w.sem, 16)
            for dst, n in ((vec, "vec"), (posb, "pos"), (cv[:, 0, :], "cb"), (mb2, "mb2"), (eb2, "eb2"),
                           (ident, "ident"), (earlier, "earlier")):
                sp.dma_start(dst[:] if dst is not None else dst, dram[n]).then_inc(s_c.sem, 16)

            def group(g, first):
                if not first:
                    sp.wait_ge(s_conv.sem, s_conv.at(g - 1))
                sp.dma_start(xp[:], dram["patches"][g, :, :, :]).then_inc(s_xp.sem, 16)
                if not first:
                    sp.wait_ge(s_h1x.sem, s_h1x.at(g - 1))
                sp.dma_start(h0[:], dram["txt"][g, :, :, :]).then_inc(s_txt.sem, 16)
                sp.wait_ge(s_txt.sem, s_txt.at(g))
                sp.wait_ge(e_conv.sem, e_conv.at(g))
                for b in range(GB):
                    t, r = divmod(b * L, 128)
                    sp.dma_start(h0[r:r + NP, t, :], cv[NP * (b % 2):NP * (b % 2) + NP, b // 2, :]
                                 ).then_inc(s_place.sem, 16)
                sp.wait_ge(e_xpj.sem, e_xpj.at(g))
                for s in range(S):
                    if s >= NROW:
                        sp.wait_ge(s_bc.sem, s_bc.at(g, s - NROW + 1))
                    elif not first:
                        sp.wait_ge(s_bc.sem, s_bc.at(g - 1))
                    row = brows[32 * (s % NROW):32 * (s % NROW) + 1, :]
                    sp.dma_start(row[:, 0:N], xd[R + s:R + s + 1, :]).then_inc(s_row[s % NROW].sem, 16)
                    sp.dma_start(row[:, N:2 * N], xd[R + S + s:R + S + s + 1, :]).then_inc(s_row[s % NROW].sem, 16)
                if not first:
                    store(g - 1)

            def store(g):
                for t, (t0, rows) in enumerate(TILES):
                    sp.wait_ge(e_e2.sem, e_e2.at(g, (NEXP - 1) * NT + t + 1))
                    sp.dma_start(out[g, t0:t0 + rows, :], acc2[0:rows, t, :]).then_inc(s_out.sem, 16)

            group(0, True)
            with sp.Fori(1, G) as g:
                group(g, False)
            store(G - 1)
            sp.wait_ge(s_out.sem, s_out.at(G - 1))

        @block.tensor
        def _(pe):
            def mm(*a, **k):
                return nc.tensor.matmul(*a, **k)

            def transposes(g, k):
                for t, (t0, rows) in enumerate(TILES):
                    if k != 3:
                        pe.wait_ge(s_norm.sem, s_norm.at(g, min(k, 3) * NT + t + 1))
                    src = xa if k == 3 else hn
                    hold(pe, "pe")
                    bank0 = P[:, 0, t0:t0 + rows] if t < 4 else P[:, 2, 0:rows]
                    bank1 = P[0:E1, 1, t0:t0 + rows] if t < 4 else P[0:E1, 2, 64:64 + rows]
                    nc.tensor.transpose(bank0, src[0:rows, t, 0:128], ident[0:rows, 0:rows])
                    last = nc.tensor.transpose(bank1, src[0:rows, t, 128:E], ident[0:rows, 0:rows])
                    if t in (3, 4):
                        last.then_inc(s_tr.sem, 1)

            def to_tokens(g, k, lhs, rhs, ready, done, freed, ks):
                for t, (t0, rows) in enumerate(TILES):
                    if t >= 4:
                        pe.wait_ge(freed.sem, freed.at(g, t - 3))
                    for j, (kt, kr) in enumerate(ks):
                        last = mm(P[0:rows, t % 4, 0:E], lhs[0:kr, kt, t0:t0 + rows], rhs[0:kr, kt, :],
                                  start=(j == 0), stop=(j == len(ks) - 1))
                    last.then_inc(done.sem, 1)

            def k2(bank, w, m, c, src=None, k1=E1):
                src = hT if src is None else src
                mm(bank, w[:, 0, 128 * m:128 * m + 128], src[:, 0, CH * c:CH * c + CH], start=True, stop=False)
                return mm(bank, w[0:k1, 1, 128 * m:128 * m + 128], src[0:k1, 1, CH * c:CH * c + CH],
                          start=False, stop=True)

            def front_a(g, first):
                pe.wait_ge(s_xp.sem, s_xp.at(g))
                if not first:
                    pe.wait_ge(e_b2.sem, e_b2.at(g - 1))
                for t in range(2):
                    for kt in range(KC):
                        last = mm(P[:, t, 0:E], xp[:, kt, 128 * t:128 * t + 128], W["cw"][:, kt, :],
                                  start=(kt == 0), stop=(kt == KC - 1))
                    last.then_inc(s_conv.sem, 1)
                pe.wait_ge(e_conv.sem, e_conv.at(g))
                transposes(g, 0)
                pe.wait_ge(e_tr.sem, e_tr.at(g, 4))
                for u in range(2 * MD):
                    m, c = divmod(u, 2)
                    if u >= 2:
                        pe.wait_ge(e_z.sem, e_z.at(g, u - 1))
                    k2(P[:, 4 + 2 * (u % 2), 0:CH], W["win"], m, c)
                    k2(P[:, 5 + 2 * (u % 2), 0:CH], W["wgate"], m, c).then_inc(s_zg.sem, 1)
                pe.wait_ge(e_z.sem, e_z.at(g))
                for c in range(2):
                    for kt in range(MD):
                        last = mm(P[:, c, 0:CH], W["wxp"][:, kt, :], zu[:, kt, CH * c:CH * c + CH],
                                  start=(kt == 0), stop=(kt == MD - 1))
                    last.then_inc(s_xpj.sem, 1)
                pe.wait_ge(e_xpj.sem, e_xpj.at(g))
                for u in range(2 * MD):
                    m, c = divmod(u, 2)
                    mm(P[:, 2 + u, 0:CH], W["wdt"][0:R, 0, 128 * m:128 * m + 128],
                       xd[0:R, CH * c:CH * c + CH], start=True, stop=True).then_inc(s_dtp.sem, 1)

            def experts(g):
                for j in range(48):
                    e, r = divmod(j, 12)
                    m, c = divmod(r, 2)
                    if j >= BURST:
                        pe.wait_ge(e_e1.sem, e_e1.at(g, j - BURST + 1))
                    k2(P[:, j % BURST, 0:CH], W["ew1"][:, 2 * e:2 * e + 2, :], m, c, xmT).then_inc(s_e1.sem, 1)
                    if r == 5 and e >= 1:
                        expert_out(g, e - 1)
                expert_out(g, NEXP - 1)

            def expert_out(g, e):
                pe.wait_ge(e_e1.sem, e_e1.at(g, 12 * e + 12))
                for t, (t0, rows) in enumerate(TILES):
                    n = e * NT + t
                    if n >= 2:
                        pe.wait_ge(e_e2.sem, e_e2.at(g, n - 1))
                    for kt in range(MM):
                        last = mm(P[0:rows, 6 + n % 2, 0:E], ge[:, kt, t0:t0 + rows],
                                  W["ew2"][:, e * MM + kt, :], start=(kt == 0), stop=(kt == MM - 1))
                    last.then_inc(s_e2.sem, 1)

            def scores(g, b):
                for i in range(4):
                    q, hg = divmod(i, 2)
                    x = score_unit(b, 0, i)
                    free_unit(g, x)
                    q0, qr = LH[q]
                    for h in unit_heads(hg):
                        p0 = HP * (h % 4)
                        col = (h // 4) * L
                        last = mm(P[0:qr, 2 * (x % 3) + h % 2, col:col + L],
                                  qT[p0:p0 + HP, h // 4, b * L + q0:b * L + q0 + qr],
                                  kT[p0:p0 + HP, h // 4, b * L:b * L + L], start=True, stop=True)
                    last.then_inc(s_S.sem, 1)

            def unit_heads(hg):
                return [4 * c + 2 * hg + a for c in range(MH) for a in range(2)]

            def score_unit(b, kind, i):
                return 8 * b + 4 * kind + i

            def free_unit(g, x):
                if x >= 3:
                    b, r = divmod(x - 3, 8)
                    if r < 4:
                        pe.wait_ge(e_S.sem, e_S.at(g, 4 * b + r + 1))
                    else:
                        pe.wait_ge(e_S2.sem, e_S2.at(g, 4 * b + r - 4 + 1))

            def scores_t(g, b):
                for i in range(4):
                    kh, hg = divmod(i, 2)
                    x = score_unit(b, 1, i)
                    free_unit(g, x)
                    k0, kr = LH[kh]
                    for h in unit_heads(hg):
                        p0 = HP * (h % 4)
                        col = (h // 4) * L
                        last = mm(P[0:kr, 2 * (x % 3) + h % 2, col:col + L],
                                  kT[p0:p0 + HP, h // 4, b * L + k0:b * L + k0 + kr],
                                  qa[p0:p0 + HP, h // 4, b * L:b * L + L], start=True, stop=True)
                    last.then_inc(s_S2.sem, 1)

            def attention(g):
                pe.wait_ge(e_qk.sem, e_qk.at(g))
                pe.wait_ge(e_v.sem, e_v.at(g))
                scores(g, 0)
                for b in range(GB):
                    pe.wait_ge(e_S.sem, e_S.at(g, 4 * b + 4))
                    if b:
                        pe.wait_ge(e_cT.sem, e_cT.at(g, 2 * b))
                    for q, (q0, qr) in enumerate(LH):
                        for m in range(MH):
                            last = nc.tensor.transpose(P[:, 6, m * L + q0:m * L + q0 + qr],
                                                       negm[0:qr, q, 128 * m:128 * m + 128], ident[0:qr, 0:qr])
                    last.then_inc(s_nm.sem, 1)
                    pe.wait_ge(e_nm.sem, e_nm.at(g, b + 1))
                    scores_t(g, b)
                    if b + 1 < GB:
                        scores(g, b + 1)
                    if b:
                        pe.wait_ge(e_cx.sem, e_cx.at(g, 2 * b))
                    pe.wait_ge(e_S2.sem, e_S2.at(g, 4 * b + 4))
                    for q, (q0, qr) in enumerate(LH):
                        for h in range(H):
                            for kh, (k0, kr) in enumerate(LH):
                                col = 256 * q + VW * h
                                last = mm(P[0:qr, 7, col:col + VW], pT[0:kr, kh * H + (h % 4) * MH + h // 4, q0:q0 + qr],
                                          vaug[0:kr, 2 * b + kh, VW * h:VW * h + VW],
                                          start=(kh == 0), stop=(kh == 1))
                    last.then_inc(s_cx.sem, 1)
                    pe.wait_ge(e_cx.sem, e_cx.at(g, 2 * b + 2))
                    for q, (q0, qr) in enumerate(LH):
                        nc.tensor.transpose(P[:, 6, q0:q0 + qr], ctxr(q)[0:qr, 0:128], ident[0:qr, 0:qr])
                        last = nc.tensor.transpose(P[0:E1, 6, 256 + q0:256 + q0 + qr], ctxr(q)[0:qr, 128:E],
                                                   ident[0:qr, 0:qr])
                    last.then_inc(s_cT.sem, 1)

            def front_b(g, moe_before):
                if moe_before:
                    pe.wait_ge(e_e2.sem, e_e2.at(g - 1))
                pe.wait_ge(s_add.sem, s_add.at(g))
                to_tokens(g, 0, acc, W["wout"], None, s_wo, e_wo, [(k, 128) for k in range(MD)])
                pe.wait_ge(e_wo.sem, e_wo.at(g))
                transposes(g, 1)
                pe.wait_ge(e_tr.sem, e_tr.at(g, 8))
                for u in range(2 * MF):
                    m, c = divmod(u, 2)
                    if u >= 2:
                        pe.wait_ge(e_gu.sem, e_gu.at(g, u - 1))
                    k2(P[:, 4 + 2 * (u % 2), 0:CH], W["wgf"], m, c)
                    k2(P[:, 5 + 2 * (u % 2), 0:CH], W["wup"], m, c).then_inc(s_gu.sem, 1)
                pe.wait_ge(e_gu.sem, e_gu.at(g))
                to_tokens(g, 0, gf, W["wdn"], None, s_wd, e_wd, [(k, 128) for k in range(MF)])
                pe.wait_ge(e_wd.sem, e_wd.at(g))
                transposes(g, 2)
                pe.wait_ge(e_tr.sem, e_tr.at(g, 12))
                for u in range(4 * MH):
                    m, c = divmod(u % (2 * MH), 2)
                    if u >= 4:
                        pe.wait_ge(e_qk.sem, e_qk.at(g, u - 3))
                    k2(P[:, 4 + u % 4, 0:CH], W["wq"] if u < 2 * MH else W["wk"], m, c).then_inc(s_qk.sem, 1)
                for u in range(2 * GB):
                    b, kh = divmod(u, 2)
                    k0, kr = LH[kh]
                    if u >= 4:
                        pe.wait_ge(e_v.sem, e_v.at(g, u - 3))
                    mm(P[0:kr, u % 4, 0:E], hT[:, 0, b * L + k0:b * L + k0 + kr], W["wv"][:, 0, :],
                       start=True, stop=False)
                    mm(P[0:kr, u % 4, 0:E], hT[0:E1 + 1, 1, b * L + k0:b * L + k0 + kr], W["wv"][0:E1 + 1, 1, :],
                       start=False, stop=True).then_inc(s_v.sem, 1)
                attention(g)
                pe.wait_ge(e_cT.sem, e_cT.at(g))
                to_tokens(g, 0, hT, W["wo"], None, s_ow, e_ow, [(0, 128), (1, E1 + 1)])
                pe.wait_ge(e_ow.sem, e_ow.at(g))
                transposes(g, 3)
                pe.wait_ge(e_tr.sem, e_tr.at(g, 16))
                for u in range(2 * MM):
                    m, c = divmod(u, 2)
                    if u >= 4:
                        pe.wait_ge(e_m1.sem, e_m1.at(g, u - 3))
                    k2(P[:, 4 + u % 4, 0:CH], W["mw1"], m, c).then_inc(s_m1.sem, 1)
                pe.wait_ge(e_m1.sem, e_m1.at(g))
                to_tokens(g, 0, g1, W["mw2"], None, s_m2, e_m2, [(k, 128) for k in range(MM)])
                pe.wait_ge(e_m2.sem, e_m2.at(g))
                transposes(g, 4)
                pe.wait_ge(e_tr.sem, e_tr.at(g, 20))
                for t, (t0, rows) in enumerate(TILES):
                    mm(P[0:rows, 4, NEXP * t:NEXP * t + NEXP], xmT[:, 0, t0:t0 + rows], W["gw"][:, 0, :],
                       start=True, stop=False)
                    last = mm(P[0:rows, 4, NEXP * t:NEXP * t + NEXP], xmT[0:E1 + 1, 1, t0:t0 + rows],
                              W["gw"][0:E1 + 1, 1, :], start=False, stop=True)
                last.then_inc(s_lg.sem, 1)
                pe.wait_ge(s_cmb.sem, s_cmb.at(g))
                for t, (t0, rows) in enumerate(TILES):
                    dst = P[0:NEXP, 5, t0:t0 + rows] if t < 4 else P[0:NEXP, 6, 0:rows]
                    last = nc.tensor.transpose(dst, comb[0:rows, t, :], ident[0:rows, 0:rows])
                    if t in (3, 4):
                        last.then_inc(s_cbT.sem, 1)
                pe.wait_ge(e_cbT.sem, e_cbT.at(g))
                for t, (t0, rows) in enumerate(TILES):
                    if t >= 4:
                        pe.wait_ge(e_b2.sem, e_b2.at(g, t - 3))
                    mm(P[0:rows, t % 4, 0:E], combT[:, t0:t0 + rows], eb2[:, :], start=True,
                       stop=True).then_inc(s_b2.sem, 1)

            pe.wait_ge(s_w.sem, 16 * len(ORDER))
            pe.wait_ge(s_c.sem, 16 * 7)
            pe.wait_ge(s_setup.sem, SETUP)
            front_a(0, True)
            front_b(0, False)
            with pe.Fori(1, G) as g:
                front_a(g, False)
                pe.wait_ge(e_dt.sem, e_dt.at(g))
                experts(g - 1)
                front_b(g, True)
            pe.wait_ge(e_b2.sem, e_b2.at(G - 1))
            experts(G - 1)

        @block.scalar
        def _(act):
            chain = Chain(c_act, act)

            def A(out_, in_, func, **k):
                return nc.scalar.activation(out_, in_, func, **k)

            def evac_transposed(g, k, dst, scale, bias):
                parts = [(0, P[:, 0, 0:512], dst[:, 0, 0:512], 0, 128), (0, P[0:E1, 1, 0:512], dst[0:E1, 1, 0:512], 1, E1),
                         (1, P[:, 2, 0:N - 512], dst[:, 0, 512:N], 0, 128),
                         (1, P[0:E1, 2, 64:64 + N - 512], dst[0:E1, 1, 512:N], 1, E1)]
                for late, src, d, slab, rows in parts:
                    act.wait_ge(s_tr.sem, s_tr.at(g, 2 * k + 1 + late))
                    kw = {}
                    if scale:
                        kw["scale"] = V(scale, slab, rows)
                    if bias:
                        kw["bias"] = V(bias, slab, rows)
                    A(d, src, ACT.Identity, **kw).then_inc(e_tr.sem, 1)

            def front_a(g, first):
                chain.begin(g)
                evac_transposed(g, 0, hT, "w1n", None)
                for u in range(2 * MD):
                    m, c = divmod(u, 2)
                    act.wait_ge(s_zg.sem, s_zg.at(g, u + 1))
                    if u >= 2:
                        act.wait_ge(e_z.sem, e_z.at(g, u - 1))
                    A(tanh_of(u), P[:, 5 + 2 * (u % 2), 0:CH], ACT.Tanh, scale=0.5).then_inc(s_tanh.sem, 1)
                for c in range(2):
                    act.wait_ge(s_xpj.sem, s_xpj.at(g, c + 1))
                    A(xd[:, CH * c:CH * c + CH], P[:, c, 0:CH], ACT.Copy).then_inc(e_xpj.sem, 1)
                for u in range(2 * MD):
                    m, c = divmod(u, 2)
                    act.wait_ge(s_dtc.sem, s_dtc.at(g, u + 1))
                    chain.link(A(dt[:, m, CH * c:CH * c + CH], dt[:, m, CH * c:CH * c + CH], ACT.Exp))
                for u in range(2 * MD):
                    m, c = divmod(u, 2)
                    A(dt[:, m, CH * c:CH * c + CH], dt[:, m, CH * c:CH * c + CH], ACT.Ln, bias=1.0
                      ).then_inc(s_sp.sem, 1)
                chain.end()

            def decay(g, j, first):
                s, m = divmod(j, MD)
                if j < MD:
                    act.wait_ge(e_dt.sem, e_dt.at(g, 2 * m + 2))
                if j == 0:
                    act.wait_ge(s_rst.sem, s_rst.at(g))
                if j >= NABAR:
                    act.wait_ge(s_h.sem, s_h.at(g, j - NABAR + 1))
                A(padded(abar[:, j % NABAR, :]), tok(dt[:, m, :]), ACT.Exp,
                  scale=negA[:, m * S + s:m * S + s + 1]).then_inc(s_ab.sem, 1)

            def hidden(g, j):
                e, r = divmod(j, 12)
                m, c = divmod(r, 2)
                act.wait_ge(s_e1.sem, s_e1.at(g, j + 1))
                if e and r == 0:
                    act.wait_ge(s_e2.sem, s_e2.at(g, e * NT))
                if e == 0 and r == 0:
                    pass
                A(ge[:, m, CH * c:CH * c + CH], P[:, j % BURST, 0:CH], ACT.Gelu,
                  bias=V("eb1", e * MM + m)).then_inc(e_e1.sem, 1)

            def scan_and_experts(g, scan, ge_group):
                for k in range(NB):
                    if scan:
                        for j in range(BURST * k, BURST * k + BURST):
                            decay(g, j, False)
                    if ge_group is not None:
                        for j in range(BURST * k, BURST * k + BURST):
                            hidden(ge_group, j)

            def front_b(g):
                evac_transposed(g, 1, hT, "wfn", None)
                for u in range(2 * MF):
                    act.wait_ge(s_gu.sem, s_gu.at(g, u + 1))
                    if u >= 2:
                        act.wait_ge(e_gu.sem, e_gu.at(g, u - 1))
                    A(tanh_of(u), P[:, 4 + 2 * (u % 2), 0:CH], ACT.Tanh, scale=0.5).then_inc(s_tg.sem, 1)
                evac_transposed(g, 2, hT, "g1", "b1")
                for b in range(GB):
                    for i in range(4):
                        kh, hg = divmod(i, 2)
                        x = 8 * b + 4 + i
                        k0, kr = LH[kh]
                        act.wait_ge(s_S2.sem, s_S2.at(g, 4 * b + i + 1))
                        if b and i == 0:
                            act.wait_ge(s_cx.sem, s_cx.at(g, b))
                        dst = pT[0:kr, kh * H + 6 * hg:kh * H + 6 * hg + 6, :].rearrange("p (a c) l -> p a (c l)", a=2)
                        A(dst, P[0:kr, 2 * (x % 3):2 * (x % 3) + 2, 0:3 * L], ACT.Exp).then_inc(e_S2.sem, 1)
                evac_transposed(g, 3, hT, None, None)
                for u in range(2 * MM):
                    m, c = divmod(u, 2)
                    act.wait_ge(s_m1.sem, s_m1.at(g, u + 1))
                    A(g1[:, m, CH * c:CH * c + CH], P[:, 4 + u % 4, 0:CH], ACT.Gelu, bias=V("mb1", m)
                      ).then_inc(e_m1.sem, 1)
                evac_transposed(g, 4, xmT, "g2", "b2")
                act.wait_ge(s_mx.sem, s_mx.at(g))
                A(gs[:, 2, :], gs[:, 1, :], ACT.Exp).then_inc(s_ex.sem, 1)

            act.wait_ge(s_c.sem, 16 * 7)
            act.wait_ge(s_setup.sem, SETUP)
            A(negA[:], vec[:, VEC["alog"][0]:VEC["alog"][0] + MD * S], ACT.Exp).then_inc(s_negA.sem, 1)
            act.wait_ge(s_negA.sem, 2)
            front_a(0, True)
            scan_and_experts(0, True, None)
            front_b(0)
            with act.Fori(1, G) as g:
                front_a(g, False)
                scan_and_experts(g, True, g - 1)
                front_b(g)
            scan_and_experts(0, False, G - 1)

        @block.vector
        def _(dve):
            chain = Chain(c_dve, dve)
            link = chain.link
            T = nc.vector

            def moments(src, g, k):
                for t, (t0, rows) in enumerate(TILES):
                    ins = T.bn_stats(stats[0:rows, t, :], src[0:rows, t, :])
                link(ins)
                hold(dve, "dve")
                for t, (t0, rows) in enumerate(TILES):
                    ins = T.bn_aggr(mv[0:rows, t, :], stats[0:rows, t, :])
                ins.then_inc(s_mv.sem, 1)
                dve.wait_ge(s_sc.sem, s_sc.at(g, k + 1))

            def scaled(dst, src, col, rows, t, centre=True):
                s = sm[0:rows, col, t:t + 1]
                if centre:
                    return T.tensor_scalar(dst[0:rows, t, :], src[0:rows, t, :], mv[0:rows, t, 0:1], s,
                                           ALU.subtract, ALU.mult)
                return T.tensor_scalar(dst[0:rows, t, :], src[0:rows, t, :], s, None, ALU.mult)

            def plus_psum(g, dst, src, done, evac):
                for t, (t0, rows) in enumerate(TILES):
                    dve.wait_ge(done.sem, done.at(g, t + 1))
                    T.tensor_tensor(dst[0:rows, t, :], src[0:rows, t, :], P[0:rows, t % 4, 0:E], ALU.add
                                    ).then_inc(evac.sem, 1)
                dve.wait_ge(evac.sem, evac.at(g))

            def front_a(g, first):
                chain.begin(g)
                for t in range(2):
                    dve.wait_ge(s_conv.sem, s_conv.at(g, t + 1))
                    if not first and t == 0:
                        dve.wait_ge(s_place.sem, s_place.at(g - 1))
                    T.tensor_tensor(cv[:, t, :], P[:, t, 0:E], posb[:], ALU.add).then_inc(e_conv.sem, 1)
                dve.wait_ge(s_place.sem, s_place.at(g))
                moments(h0, g, 0)
                for t, (t0, rows) in enumerate(TILES):
                    scaled(xa, h0, 2, rows, t)
                    scaled(hn, h0, 6, rows, t).then_inc(s_norm.sem, 1)
                dve.wait_ge(s_norm.sem, s_norm.at(g, NT))
                for u in range(2 * MD):
                    m, c = divmod(u, 2)
                    dve.wait_ge(s_tanh.sem, s_tanh.at(g, u + 1))
                    T.scalar_tensor_tensor(out=zu[:, m, CH * c:CH * c + CH], in0=tanh_of(u), scalar=1.0,
                                           in1=P[:, 4 + 2 * (u % 2), 0:CH], op0=ALU.add, op1=ALU.mult
                                           ).then_inc(e_z.sem, 1)
                for u in range(2 * MD):
                    m, c = divmod(u, 2)
                    dve.wait_ge(s_dtp.sem, s_dtp.at(g, u + 1))
                    T.tensor_scalar(dt[:, m, CH * c:CH * c + CH], P[:, 2 + u, 0:CH], V("bdt", m), SPC,
                                    ALU.add, ALU.min).then_inc(s_dtc.sem, 1)
                for u in range(2 * MD):
                    m, c = divmod(u, 2)
                    dve.wait_ge(s_sp.sem, s_sp.at(g, u + 1))
                    v = dt[:, m, CH * c:CH * c + CH]
                    T.scalar_tensor_tensor(out=v, in0=P[:, 2 + u, 0:CH], scalar=V("bdt", m), in1=v,
                                           op0=ALU.add, op1=ALU.max).then_inc(e_dt.sem, 1)
                dve.wait_ge(e_dt.sem, e_dt.at(g))
                for m in range(MD):
                    T.tensor_scalar(acc[:, m, :], zu[:, m, :], V("dsk", m), None, ALU.mult).then_inc(s_acc0.sem, 1)
                link(T.memset(abar[:, :, :].rearrange("p a (b l) -> p a b l", l=LP)[:, :, :, 0:1], 0.0))
                T.memset(ring[:, :, :].rearrange("p a (b l) -> p a b l", l=LP)[:, :, :, 0:1], 0.0).then_inc(s_rst.sem, 1)
                dve.wait_ge(s_acc0.sem, s_acc0.at(g))
                for m in range(MD):
                    ins = T.tensor_tensor(zu[:, m, :], zu[:, m, :], dt[:, m, :], ALU.mult)
                link(ins)

            def bx(g, j, first):
                s, m = divmod(j, MD)
                if j == 0:
                    dve.wait_ge(s_rst.sem, s_rst.at(g))
                if m == 0:
                    dve.wait_ge(s_bc.sem, s_bc.at(g, s + 1))
                if j >= NRING:
                    dve.wait_ge(s_add.sem, s_add.at(g, j - NRING + 1))
                T.tensor_tensor(padded(ring[:, j % NRING, :]), tok(zu[:, m, :]), tok(bc[:, s % NBC, 0:N]),
                                ALU.mult).then_inc(s_bx.sem, 1)

            def scan(g, j):
                dve.wait_ge(s_bx.sem, s_bx.at(g, j + 1))
                dve.wait_ge(s_ab.sem, s_ab.at(g, j + 1))
                v = ring[:, j % NRING, :]
                T.tensor_tensor_scan(v, abar[:, j % NABAR, :], v, 0.0, ALU.mult, ALU.add).then_inc(s_h.sem, 1)

            def hc(g, j):
                s, m = divmod(j, MD)
                dve.wait_ge(s_h.sem, s_h.at(g, j + 1))
                v = padded(ring[:, j % NRING, :])
                T.tensor_tensor(v, v, tok(bc[:, s % NBC, N:2 * N]), ALU.mult).then_inc(s_hc.sem, 1)

            def expert_add(g, n):
                e, t = divmod(n, NT)
                rows = TILES[t][1]
                dve.wait_ge(s_e2.sem, s_e2.at(g, n + 1))
                if e:
                    dve.wait_ge(e_e2.sem, e_e2.at(g, n - NT + 1))
                else:
                    dve.wait_ge(e_b2.sem, e_b2.at(g))
                T.scalar_tensor_tensor(out=acc2[0:rows, t, :], in0=P[0:rows, 6 + n % 2, 0:E],
                                       scalar=comb[0:rows, t, e:e + 1], in1=acc2[0:rows, t, :],
                                       op0=ALU.mult, op1=ALU.add).then_inc(e_e2.sem, 1)

            def scan_and_experts(g, ge_group):
                for j in range(STEPS + 2):
                    if j < STEPS:
                        bx(g, j, False)
                    if 1 <= j <= STEPS:
                        scan(g, j - 1)
                    if j >= 2:
                        hc(g, j - 2)
                    if ge_group is not None and j >= 14 and (j - 14) % 12 < NT and j < STEPS:
                        expert_add(ge_group, (j - 14) // 12 * NT + (j - 14) % 12)
                if ge_group is not None:
                    for t in range(NT):
                        expert_add(ge_group, (NEXP - 1) * NT + t)

            def front_b(g):
                plus_psum(g, xa, xa, s_wo, e_wo)
                moments(xa, g, 1)
                for t, (t0, rows) in enumerate(TILES):
                    scaled(hn, xa, 2, rows, t, centre=False).then_inc(s_norm.sem, 1)
                for t, (t0, rows) in enumerate(TILES):
                    ins = T.tensor_tensor(h0[0:rows, t, :], h0[0:rows, t, :], xa[0:rows, t, :], ALU.add)
                link(ins)
                for u in range(2 * MF):
                    m, c = divmod(u, 2)
                    dve.wait_ge(s_tg.sem, s_tg.at(g, u + 1))
                    v = gf[:, m, CH * c:CH * c + CH]
                    link(T.scalar_tensor_tensor(out=v, in0=tanh_of(u), scalar=1.0,
                                                in1=P[:, 4 + 2 * (u % 2), 0:CH], op0=ALU.add, op1=ALU.mult))
                    T.tensor_tensor(v, v, P[:, 5 + 2 * (u % 2), 0:CH], ALU.mult).then_inc(e_gu.sem, 1)
                plus_psum(g, h0, h0, s_wd, e_wd)
                moments(h0, g, 2)
                for t, (t0, rows) in enumerate(TILES):
                    scaled(xa, h0, 2, rows, t)
                    scaled(hn, h0, 6, rows, t).then_inc(s_norm.sem, 1)
                for u in range(4 * MH):
                    m, c = divmod(u % (2 * MH), 2)
                    dve.wait_ge(s_qk.sem, s_qk.at(g, u + 1))
                    src = P[:, 4 + u % 4, 0:CH]
                    if u < 2 * MH:
                        ins = T.tensor_scalar(qT[:, m, CH * c:CH * c + CH], src, V("qb", m), HD ** -0.5,
                                              ALU.add, ALU.mult)
                    else:
                        ins = T.tensor_scalar(kT[:, m, CH * c:CH * c + CH], src, V("kb", m), None, ALU.add)
                    ins.then_inc(e_qk.sem, 1)
                link(T.memset(vaug[:, :, :].rearrange("p a (h w) -> p a h w", w=VW)[:, :, :, HD:VW], 1.0))
                for u in range(2 * GB):
                    b, kh = divmod(u, 2)
                    kr = LH[kh][1]
                    dve.wait_ge(s_v.sem, s_v.at(g, u + 1))
                    T.tensor_copy(vaug[0:kr, u, :].rearrange("p (h w) -> p h w", w=VW)[:, :, 0:HD],
                                  P[0:kr, u % 4, 0:E].rearrange("p (h w) -> p h w", w=HD)).then_inc(e_v.sem, 1)

                def maxima(b):
                    for i in range(4):
                        q, hg = divmod(i, 2)
                        qr = LH[q][1]
                        x = 8 * b + i
                        dve.wait_ge(s_S.sem, s_S.at(g, 4 * b + i + 1))
                        if b and i == 0:
                            dve.wait_ge(s_nm.sem, s_nm.at(g, b))
                        dst = negm[0:qr, q, :].rearrange("p (c r w) -> p r c w", r=4, w=HP)[:, 2 * hg:2 * hg + 2, :, HD]
                        src = P[0:qr, 2 * (x % 3):2 * (x % 3) + 2, 0:3 * L].rearrange("p a (c l) -> p a c l", l=L)
                        T.tensor_reduce(dst, src, AX.X, ALU.max,
                                        negate=True).then_inc(e_S.sem, 1)

                maxima(0)
                for b in range(GB):
                    dve.wait_ge(s_nm.sem, s_nm.at(g, b + 1))
                    T.tensor_tensor(qa[:, :, b * L:b * L + L], qT[:, :, b * L:b * L + L],
                                    P[:, 6, 0:MH * L].rearrange("p (m l) -> p m l", m=MH), ALU.add
                                    ).then_inc(e_nm.sem, 1)
                    if b + 1 < GB:
                        maxima(b + 1)
                    dve.wait_ge(s_cx.sem, s_cx.at(g, b + 1))
                    for q, (q0, qr) in enumerate(LH):
                        src = P[0:qr, 7, 256 * q:256 * q + H * VW].rearrange("p (h w) -> p h w", w=VW)
                        rs = gs[0:qr, 6 + q, 0:H]
                        link(T.reciprocal(rs, src[:, :, HD:VW].rearrange("p h w -> p (h w)")))
                        T.tensor_tensor(ctxr(q)[0:qr, :].rearrange("p (h w) -> p h w", w=HD), src[:, :, 0:HD],
                                        rs.unsqueeze(2).to_broadcast([qr, H, HD]), ALU.mult
                                        ).then_inc(e_cx.sem, 1)
                    dve.wait_ge(s_cT.sem, s_cT.at(g, b + 1))
                    T.tensor_copy(hT[:, 0, b * L:b * L + L], P[:, 6, 0:L]).then_inc(e_cT.sem, 1)
                    T.tensor_copy(hT[0:E1, 1, b * L:b * L + L], P[0:E1, 6, 256:256 + L]).then_inc(e_cT.sem, 1)
                for t, (t0, rows) in enumerate(TILES):
                    dve.wait_ge(s_ow.sem, s_ow.at(g, t + 1))
                    T.tensor_tensor(xa[0:rows, t, :], xa[0:rows, t, :], P[0:rows, t % 4, 0:E], ALU.add
                                    ).then_inc(e_ow.sem, 1)
                dve.wait_ge(e_ow.sem, e_ow.at(g))
                for t, (t0, rows) in enumerate(TILES):
                    dve.wait_ge(s_m2.sem, s_m2.at(g, t + 1))
                    dve.wait_ge(s_x5b.sem, s_x5b.at(g, t + 1))
                    T.tensor_tensor(hn[0:rows, t, :], hn[0:rows, t, :], P[0:rows, t % 4, 0:E], ALU.add
                                    ).then_inc(e_m2.sem, 1)
                dve.wait_ge(e_m2.sem, e_m2.at(g))
                moments(hn, g, 3)
                dve.wait_ge(s_h1x.sem, s_h1x.at(g))
                for t, (t0, rows) in enumerate(TILES):
                    scaled(hn, hn, 2, rows, t).then_inc(s_norm.sem, 1)
                dve.wait_ge(s_lg.sem, s_lg.at(g))
                lg = gs[:, 0, :]
                link(T.tensor_copy(gs[:, 0, 0:4 * NEXP], P[:, 4, 0:4 * NEXP]))
                rl = TILES[-1][1]
                link(T.tensor_copy(gs[0:rl, 0, 4 * NEXP:NT * NEXP], P[0:rl, 4, 4 * NEXP:NT * NEXP]))
                l3 = lg.rearrange("p (t e) -> p t e", t=NT)
                link(T.tensor_reduce(gm[:, 0, :], l3, AX.X, ALU.max))
                T.tensor_tensor(gs[:, 1, :].rearrange("p (t e) -> p t e", t=NT), l3,
                                gm[:, 0, :].unsqueeze(2).to_broadcast([128, NT, NEXP]), ALU.subtract
                                ).then_inc(s_mx.sem, 1)
                for e in range(NEXP):
                    le = l3[:, :, e:e + 1].to_broadcast([128, NT, NEXP])
                    gt = gr[:, 0, :, NEXP * e:NEXP * e + NEXP]
                    eq = gr[:, 1, :, NEXP * e:NEXP * e + NEXP]
                    T.tensor_tensor(gt, l3, le, ALU.is_gt)
                    ins = T.tensor_tensor(eq, l3, le, ALU.is_equal)
                link(ins)
                link(T.tensor_tensor(gr[:, 1, :, :], gr[:, 1, :, :],
                                     earlier[:, :, :].rearrange("p e j -> p (e j)").unsqueeze(1).to_broadcast(
                                         [128, NT, NEXP * NEXP]), ALU.mult))
                link(T.tensor_tensor(gr[:, 0, :, :], gr[:, 0, :, :], gr[:, 1, :, :], ALU.add))
                link(T.tensor_reduce(gs[:, 3, :].rearrange("p (t e) -> p t e", t=NT),
                                     gr[:, 0, :, :].rearrange("p t (e j) -> p t e j", e=NEXP), AX.X, ALU.add))
                dve.wait_ge(s_ex.sem, s_ex.at(g))
                link(T.scalar_tensor_tensor(out=gs[:, 4, :], in0=gs[:, 3, :], scalar=1.5, in1=gs[:, 2, :],
                                            op0=ALU.is_lt, op1=ALU.mult))
                link(T.tensor_reduce(gm[:, 1, :], gs[:, 4, :].rearrange("p (t e) -> p t e", t=NT), AX.X, ALU.add))
                link(T.reciprocal(gm[:, 2, :], gm[:, 1, :]))
                T.tensor_tensor(comb[:, :, :], gs[:, 4, :].rearrange("p (t e) -> p t e", t=NT),
                                gm[:, 2, :].unsqueeze(2).to_broadcast([128, NT, NEXP]), ALU.mult
                                ).then_inc(s_cmb.sem, 1)
                dve.wait_ge(s_cbT.sem, s_cbT.at(g, 1))
                T.tensor_copy(combT[:, 0:512], P[0:NEXP, 5, 0:512]).then_inc(e_cbT.sem, 1)
                dve.wait_ge(s_cbT.sem, s_cbT.at(g, 2))
                T.tensor_copy(combT[:, 512:N], P[0:NEXP, 6, 0:N - 512]).then_inc(e_cbT.sem, 1)
                plus_psum(g, acc2, acc2, s_b2, e_b2)
                chain.end()

            dve.wait_ge(s_w.sem, 16 * len(ORDER))
            dve.wait_ge(s_c.sem, 16 * 7)
            for ins in (T.tensor_scalar(W["win"][:], W["win"][:], 0.5, None, ALU.mult),
                        T.tensor_scalar(W["wup"][:], W["wup"][:], 0.5, None, ALU.mult),
                        T.tensor_tensor(posb[:], posb[:], cv[:, 0, :], ALU.add),
                        T.memset(hT[E1:128, 1, :], 1.0), T.memset(xmT[E1:128, 1, :], 1.0),
                        T.memset(mv[:], 1.0), T.memset(gs[:], 0.0), T.memset(comb[:], 0.0),
                        T.memset(negm[:], 0.0), T.memset(half[:], -0.5), T.memset(sm[:], 1.0),
                        T.memset(hn[:], 0.0), T.memset(xa[:], 0.0)):
                ins.then_inc(s_setup.sem, 1)
            dve.wait_ge(s_setup.sem, SETUP)
            dve.wait_ge(s_negA.sem, 1)
            T.tensor_scalar(negA[:], negA[:], -1.0, None, ALU.mult).then_inc(s_negA.sem, 1)
            front_a(0, True)
            scan_and_experts(0, None)
            front_b(0)
            with dve.Fori(1, G) as g:
                front_a(g, False)
                scan_and_experts(g, g - 1)
                front_b(g)
            for n in range(NEXP * NT):
                expert_add(G - 1, n)

        @block.gpsimd
        def _(pool):
            chain = Chain(c_pool, pool)
            link = chain.link
            Q = nc.gpsimd

            def power(dst, src):
                return Q.tensor_tensor(sm[:, dst, :], sm[:, src, :], half[:], ALU.pow)

            def scales(g, k):
                pool.wait_ge(s_mv.sem, s_mv.at(g, k + 1))
                mean, var = mv[:, :, 0], mv[:, :, 1]
                if k == 1:
                    link(Q.tensor_tensor(sm[:, 0, :], mean, mean, ALU.mult))
                    link(Q.tensor_tensor(sm[:, 0, :], sm[:, 0, :], var, ALU.add))
                    hold(pool, "pool")
                    link(Q.tensor_scalar(sm[:, 1, :], sm[:, 0, :], 1e-6, None, ALU.add))
                    power(2, 1).then_inc(s_sc.sem, 1)
                    return
                hold(pool, "pool")
                link(Q.tensor_scalar(sm[:, 1, :], var, 1e-5, None, ALU.add))
                if k == 3:
                    power(2, 1).then_inc(s_sc.sem, 1)
                    return
                link(power(2, 1))
                link(Q.tensor_tensor(sm[:, 3, :], var, sm[:, 2, :], ALU.mult))
                link(Q.tensor_tensor(sm[:, 4, :], sm[:, 3, :], sm[:, 2, :], ALU.mult))
                hold(pool, "pool")
                link(Q.tensor_scalar(sm[:, 3, :], sm[:, 4, :], 1e-6 if k == 0 else 1e-5, None, ALU.add))
                link(power(5, 3))
                Q.tensor_tensor(sm[:, 6, :], sm[:, 2, :], sm[:, 5, :], ALU.mult).then_inc(s_sc.sem, 1)

            def broadcast(g, s):
                pool.wait_ge(s_row[s % NROW].sem, s_row[s % NROW].at(g, 32 * (s // NROW + 1)))
                if s >= NBC:
                    pool.wait_ge(s_hc.sem, s_hc.at(g, MD * (s - NBC + 1)))
                elif s == 0:
                    pool.wait_ge(s_rst.sem, s_rst.at(g))
                r = 32 * (s % NROW)
                if s >= NBC:
                    pool.wait_ge(s_add.sem, s_add.at(g, MD * (s - NBC + 1)))
                hold(pool, "pool")
                Q.partition_broadcast(bc[:, s % NBC, :], brows[r:r + 1, :]).then_inc(s_bc.sem, 1)
                pool.wait_ge(s_bc.sem, s_bc.at(g, s + 1))

            def group(g, first):
                chain.begin(g)
                scales(g, 0)
                pool.wait_ge(s_acc0.sem, s_acc0.at(g))
                broadcast(g, 0)
                broadcast(g, 1)
                for j in range(STEPS):
                    s, m = divmod(j, MD)
                    pool.wait_ge(s_hc.sem, s_hc.at(g, j + 1))
                    if s:
                        pool.wait_ge(s_add.sem, s_add.at(g, j - MD + 1))
                    y = tok(acc[:, m, :])
                    Q.tensor_tensor(y, y, padded(ring[:, j % NRING, :]), ALU.add).then_inc(s_add.sem, 1)
                    if m == MD - 1 and s + NBC < S:
                        broadcast(g, s + NBC)
                for k in (1, 2):
                    scales(g, k)
                for t, (t0, rows) in enumerate(TILES):
                    pool.wait_ge(e_ow.sem, e_ow.at(g, t + 1))
                    Q.tensor_tensor(hn[0:rows, t, :], xa[0:rows, t, :], mb2[0:rows, :], ALU.add
                                    ).then_inc(s_x5b.sem, 1)
                if not first:
                    pool.wait_ge(s_out.sem, s_out.at(g - 1))
                pool.wait_ge(e_m2.sem, e_m2.at(g))
                for t, (t0, rows) in enumerate(TILES):
                    Q.tensor_tensor(acc2[0:rows, t, :], h0[0:rows, t, :], hn[0:rows, t, :], ALU.add
                                    ).then_inc(s_h1x.sem, 1)
                scales(g, 3)
                chain.end()

            pool.wait_ge(s_setup.sem, SETUP)
            pool.wait_ge(s_c.sem, 16 * 7)
            group(0, True)
            with pool.Fori(1, G) as g:
                group(g, False)


def layouts(np, i):
    f = lambda a: np.ascontiguousarray(np.asarray(a, np.float32))

    def tiles(a, m=None):
        k = -(-a.shape[0] // 128)
        out = np.zeros((k * 128, a.shape[1]), np.float32)
        out[:a.shape[0]] = a
        return out.reshape(k, 128, -1).transpose(1, 0, 2)

    def cols(v, k):
        out = np.zeros(k * 128, np.float32)
        out[:v.size] = v.reshape(-1)
        return out.reshape(k, 128).T

    def heads(a):
        out = np.zeros((H, HP) + a.shape[1:], np.float32)
        out[:, :HD] = a.reshape((H, HD) + a.shape[1:])
        return out.reshape((H * HP,) + a.shape[1:])

    w = {n: np.asarray(v) for n, v in i.items()}
    A, F = "L0_attn_", "L0_ffn_"
    x = w["x"].reshape(G, GB, C_IN, SIDE, PATCH, SIDE, PATCH).transpose(0, 2, 4, 6, 1, 3, 5)
    x = x.reshape(G, KC, 128, GB * NP).transpose(0, 2, 1, 3)
    txt = np.zeros((B, L, E), np.float32)
    txt[:, NP:] = w["txt"]
    t = np.zeros((G, NT * 128, E), np.float32)
    t[:, :N] = txt.reshape(G, N, E)
    pos = w["L0_tok_pos_table"].reshape(32, 32, E)[::32 // SIDE, ::32 // SIDE].reshape(NP, E)
    inw, inb = w[F + "in_w"], w[F + "in_b"]
    bias_row = lambda a, b: np.concatenate([a, b.reshape(1, -1)])
    kb = heads(inb[E:2 * E]).reshape(H, HP)
    kb[:, HD] = 1.0
    vecs = {"w1n": cols(w[A + "w_norm1"], 2), "wfn": cols(w[A + "w_ffn_norm"], 2),
            "g1": cols(w[F + "ln1_g"], 2), "b1": cols(w[F + "ln1_b"], 2),
            "g2": cols(w[F + "ln2_g"], 2), "b2": cols(w[F + "ln2_b"], 2),
            "bdt": cols(w[A + "b_dt"], MD), "dsk": cols(w[A + "D_skip"], MD),
            "alog": w[A + "A_log"].reshape(MD, 128, S).transpose(1, 0, 2).reshape(128, MD * S),
            "qb": cols(heads(inb[:E]), MH), "kb": cols(kb, MH), "mb1": cols(w[F + "mlp_b1"], MM),
            "eb1": w[F + "exp_b1"].reshape(NEXP * MM, 128).T}
    a = {"patches": x, "txt": t.reshape(G, NT, 128, E).transpose(0, 2, 1, 3),
         "cw": tiles(w["L0_tok_conv_w"].reshape(E, -1).T),
         "win": tiles(w[A + "W_in"].T), "wgate": tiles(w[A + "W_gate"].T), "wxp": tiles(w[A + "W_xproj"].T),
         "wdt": tiles(w[A + "W_dt"].T), "wout": tiles(w[A + "W_out"].T), "wgf": tiles(w[A + "W_gate_ffn"].T),
         "wup": tiles(w[A + "W_up"].T), "wdn": tiles(w[A + "W_down"].T),
         "wq": tiles(heads(inw[:E]).T), "wk": tiles(heads(inw[E:2 * E]).T),
         "wv": tiles(bias_row(inw[2 * E:].T, inb[2 * E:])),
         "wo": tiles(bias_row(w[F + "out_w"].T, w[F + "out_b"])),
         "mw1": tiles(w[F + "mlp_w1"]), "mw2": tiles(w[F + "mlp_w2"]),
         "gw": tiles(bias_row(w[F + "gate_w"].T, w[F + "gate_b"])),
         "ew1": np.concatenate([tiles(w[F + "exp_w1"][e]) for e in range(NEXP)], 1),
         "ew2": np.concatenate([tiles(w[F + "exp_w2"][e]) for e in range(NEXP)], 1),
         "vec": np.concatenate([vecs[n] for n in VEC], 1),
         "pos": np.concatenate([pos, pos]), "cb": np.tile(w["L0_tok_conv_b"], (128, 1)),
         "mb2": np.tile(w[F + "mlp_b2"], (128, 1)), "eb2": w[F + "exp_b2"],
         "ident": np.eye(128), "earlier": np.tile(np.tril(np.ones((NEXP, NEXP)), -1), (128, 1, 1))}
    return {n: f(v) for n, v in a.items()}


def kernel(**inputs):
    import numpy as np
    import concourse.bacc as bacc
    from concourse.bass_utils import run_bass_kernel_spmd as run

    nc = bacc.Bacc("TRN2", target_bir_lowering=False, num_devices=1)
    arrays, dram = {}, {}
    for name, a in layouts(np, inputs).items():
        arrays["in_" + name] = a
        dram[name] = nc.dram_tensor("in_" + name, a.shape, F32, kind="ExternalInput").ap()
    out = nc.dram_tensor("out", (B, L, E), F32, kind="ExternalOutput").ap()
    early_fusion_program(nc, dram, out.rearrange("(g b) l e -> g (b l) e", b=GB))
    r = run(nc, [arrays], core_ids=[0])
    return r.results[0]["out"]
```

```python
import concourse.bass as bass
from concourse import mybir
from contextlib import ExitStack

ALU = mybir.AluOpType
ACT = mybir.ActivationFunctionType
AX = mybir.AxisListType
F32 = mybir.dt.float32
F32R = mybir.dt.float32r

B, C_IN, IMG, PATCH = 32, 3, 128, 16
SIDE = IMG // PATCH
NP, NTXT = SIDE * SIDE, 77
L = NP + NTXT
E = 192
E1 = E - 128
KC = C_IN * PATCH * PATCH // 128
GB = 4
G = B // GB
N = GB * L
CH = N // 2
TILES = [(t, min(128, N - t)) for t in range(0, N, 128)]
NT = len(TILES)
DI, S, R = 384, 16, 96
MD = DI // 128
HF = 512
MF = HF // 128
H, HD = 12, E // 12
HP = 64
MH = H * HP // 128
MQ = 2 * E // 128
LE = L + 1
HID, NEXP = 768, 4
MM = HID // 128
EW = 2 * HID + MM * E
UPE = MM * 2
NU = NEXP * MM * 2
LH = [(0, 71), (71, 70)]
VW = 2 * HD
MC = H * VW // 128
LP = L + 1
NPAD = GB * LP
STEPS = S * MD
NABAR, NRING, NBC, NROW = 5, 5, 2, 4
SPC = 30.0

VEC = {}
for _name, _w in (("w1n", 2), ("wfn", 2), ("g1", 2), ("b1", 2), ("g2", 2), ("b2", 2), ("bdt", MD),
                  ("alog", MD * S), ("dsk", MD), ("mb1", MM), ("eb1", NEXP * MM), ("kone", 1)):
    VEC[_name] = (sum(w for _, w in VEC.values()), _w)
VW_ALL = sum(w for _, w in VEC.values())

WEIGHTS = {"win": (2, DI), "wgate": (2, DI), "wxp": (MD, 128), "wdt": (1, DI), "wout": (MD, E),
           "wgf": (2, HF), "wup": (2, HF), "wdn": (MF, E), "wqk": (2, 2 * E),
           "wv": (2, E), "wo": (MC, E), "mw1": (2, HID), "mw2": (MM, E), "gw": (2, NEXP)}
ORDER = list(WEIGHTS)


TO_SCAN = [0, 2, 3, 4, 5, 6, 6, 7, 8, 8, 9, 9, 9, 10, 10, 10, 10]
TO_QK = [17, 22] + [25 + u for u in range(8)] + [42] * 5 + [43, 48]
LAG = 1
DECAYS = [0, 8, 5, 5]


def free(j, d):
    return d < STEPS and (d < NABAR or d - j < NABAR - 1)


def first_phase(with_a, with_b, with_e, lag=LAG):
    a = [("norm", 0), ("tr", 0)] + [("z", u) for u in range(2 * MD)] + [("xp", c) for c in range(2)]
    a += [("dt", u) for u in range(2 * MD)] + [("dtend", 0)]
    b = [("norm", 1), ("tr", 1)] + [("gu", u) for u in range(2 * MF)] + [("dn", t) for t in range(NT)]
    b += [("norm", 2), ("tr", 2)]
    beside = (list(zip(TO_SCAN, a)) if with_a else []) + (list(zip(TO_QK, b)) if with_b else [])
    last = 0
    for n, (at, item) in enumerate(beside):
        last = max(last, at if item[0] == "norm" else at + lag)
        beside[n] = (last, item)
    if not with_e:
        return [item for _, item in beside], 0, 0
    out, j, d = [("mm", 0), ("mm", 1)], 0, 0
    for u in range(NU):
        ex, r = divmod(u, UPE)
        out.append(("act", u))
        if u + 2 < NU:
            out.append(("mm", u + 2))
        while beside and beside[0][0] == u:
            out.append(beside.pop(0)[1])
        if r % 2 == 1 and j < d:
            out.append(("scn", j))
            j += 1
        if r == UPE - 1:
            decays = DECAYS[ex] if with_a else 0
            while decays and free(j, d):
                out.append(("dec", d))
                d, decays = d + 1, decays - 1
            for t in range(NT):
                out.append(("eout", ex * NT + t))
                while ex == NEXP - 1 and beside and beside[0][0] == NU + t:
                    out.append(beside.pop(0)[1])
                for _ in range(-(-decays // (NT - t))):
                    while not free(j, d):
                        out.append(("scn", j))
                        j += 1
                    out.append(("dec", d))
                    d, decays = d + 1, decays - 1
    assert not beside
    return out, j, d


def second_phase(with_b, with_s, j=0, d=0):
    if not with_b:
        out = [("dec", 0)]
        for j in range(STEPS + 2):
            out += ([("dec", j + 1)] if j + 1 < STEPS else []) + [("scn", j)]
        return out + [("wout", 0)]
    b, want = [], []

    def add(items, steps):
        for n, it in enumerate(items):
            b.append(it)
            want.append(steps * (n + 1) // len(items) - steps * n // len(items))

    add([("qp", u) for u in range(MQ)] + [("qk", u) for u in range(2 * MH)], 5)
    add([("v", u) for u in range(4)], 1)

    def scores(q):
        return [("S", 4 * q + i) for i in range(4)]

    def scores_t(q, between=()):
        return [("nm", q)] + list(between) + [("S2", 4 * q + i) for i in range(4)]

    add(scores(0), 2)
    add(scores_t(0), 3)
    add(scores(1), 2)
    add([("ctx", 0)], 1)
    add(scores_t(1, [("sum", 0)]), 3)
    add([("qp", MQ + u) for u in range(MQ)] + [("qk", 2 * MH + u) for u in range(2 * MH)], 5)
    add([("ctx", 1)], 1)
    add([("v", 4 + u) for u in range(4)] + [("sum", 1)], 1)
    add(scores(2), 2)
    add(scores_t(2), 3)
    add(scores(3), 2)
    add([("ctx", 2)], 1)
    add(scores_t(3, [("sum", 2)]), 3)
    add([("ctx", 3), ("sum", 3)], 1)
    add([("ow", t) for t in range(NT)], 1)
    add([("tr", 3)], 0)
    add([("m1", u) for u in range(2 * MM)], 4)
    add([("m2", t) for t in range(NT)] + ([("wout", 0)] if with_s else []), 0)
    add([("norm", 3), ("tr", 4), ("gate", 0)] + [("b2", t) for t in range(NT)], 0)
    if not with_s:
        return b
    left, weight, sofar = STEPS + 2 - j, sum(want), 0
    for n, w in enumerate(list(want)):
        want[n] = left * (sofar + w) // weight - left * sofar // weight
        sofar += w
    out = []
    if d == 0:
        out, d = [("dec", 0)], 1
    for item, n in zip(b, want):
        gelu = item[0] in ("m1", "m2")
        if item == ("m1", 0):
            while free(j, d):
                out.append(("dec", d))
                d += 1
        out.append(item)
        for _ in range(n):
            if not gelu and free(j, d):
                out.append(("dec", d))
                d += 1
            assert d >= min(j, STEPS), (item, j, d)
            out.append(("scn", j))
            j += 1
    assert j == STEPS + 2 and d == STEPS
    return out


class Signal:

    def __init__(self, sem, per):
        self.sem, self.per = sem, per

    def at(self, g, k=None):
        return g * self.per + (self.per if k is None else k)


class Chain:

    def __init__(self, signal, eng):
        self.rises, self.eng, self.k, self.g = signal, eng, 0, 0

    def begin(self, g):
        self.g, self.k = g, 0

    def link(self, ins):
        self.k += 1
        ins.then_inc(self.rises.sem, 1)
        self.eng.wait_ge(self.rises.sem, self.rises.at(self.g, self.k))

    def end(self):
        assert self.k == self.rises.per, self.k


def early_fusion_program(nc, dram, out):
    tokens = nc.dram_tensor("tokens", (B, L, E), F32, kind="Internal").ap()
    with ExitStack() as ctx:
        def sb(name, *shape, dtype=F32):
            return ctx.enter_context(nc.sbuf_tensor(name, list(shape), dtype))

        def signal(name, per):
            return Signal(ctx.enter_context(nc.semaphore(name)), per)

        def norms(name, per):
            return [signal(f"{name}_{k}", per) for k in range(5)]

        W = {n: sb("w_" + n, 128, *WEIGHTS[n]) for n in ORDER}
        ew = sb("ew", 128, 2, EW)
        vec = sb("vec", 128, VW_ALL)
        ident = sb("ident", 128, 128)
        mb2 = sb("mb2", 128, E)
        eb2 = sb("eb2", NEXP, E)
        earlier = sb("earlier", 128, NEXP, NEXP)
        negA = sb("negA", 128, MD * S)
        half = sb("half", 128, NT)
        place = sb("place", 2 * H, MH, 128, dtype=F32R)
        h0n = sb("h0n", 128, NT, E)
        h0 = sb("h0", 128, NT, E)
        xa = sb("xa", 128, NT, E)
        hn = sb("hn", 128, NT, E)
        acc2 = sb("acc2", 128, NT, E)
        hT = sb("hT", 128, 2, N)
        xmT = sb("xmT", 128, 2, N)
        xd = sb("xd", 128, N)
        qr = sb("qr", 128, MH, 2, LE, dtype=F32R)
        kr = sb("kr", 128, MH, 2, LE, dtype=F32R)
        qk_hi = sb("qk_hi", 128, MQ, CH, dtype=F32R)
        qk_lo = sb("qk_lo", 128, MQ, CH, dtype=F32R)
        split = sb("split", 128, 4, 128, dtype=F32R)
        mf = sb("mf", 128, 2, H)
        mneg = sb("mneg", 128, 2, 2, H)
        mT = sb("mT", 2 * H, LE, dtype=F32R)
        stats = sb("stats", 128, NT, 6)
        mvs = [sb(f"mv{k}", 128, NT, 2) for k in range(2)]
        sms = [sb(f"sm{k}", 128, 7, NT) for k in range(2)]
        gs = sb("gs", 128, 5, NT * NEXP)
        gr = sb("gr", 128, 2, NT, NEXP * NEXP)
        gm = sb("gm", 128, 3, NT)
        comb = sb("comb", 128, NT, NEXP)
        cs = sb("cs", 128, MC, L)
        pick = sb("pick", 128, 128)
        brows = sb("brows", 128, 2 * N)
        scan_mem = sb("scan_mem", 128, 3 * MD * N + NABAR * NPAD + NRING * NPAD + NBC * 2 * N)
        ffn_mem = sb("ffn_mem", 128, MM * N + N)
        ge_mem = sb("ge_mem", 128, MM * N)

        def cut(mem, at, n, width):
            return mem[:, at:at + n * width].rearrange("p (a b) -> p a b", a=n)

        zu = cut(scan_mem, 0, MD, N)
        dt = cut(scan_mem, MD * N, MD, N)
        acc = cut(scan_mem, 2 * MD * N, MD, N)
        abar = cut(scan_mem, 3 * MD * N, NABAR, NPAD)
        cl = cut(scan_mem, 3 * MD * N, MD, N)
        ring = cut(scan_mem, 3 * MD * N + NABAR * NPAD, NRING, NPAD)
        bc = cut(scan_mem, 3 * MD * N + (NABAR + NRING) * NPAD, NBC, 2 * N)
        XPR, CVR = 4, 4
        cw = cut(scan_mem, 0, KC, E)
        xp = scan_mem[:, KC * E:KC * E + XPR * KC * 128].rearrange("p (r a b) -> p r a b", r=XPR, a=KC)
        o = KC * E + XPR * KC * 128
        cvs = cut(scan_mem, o, CVR, E)
        posb = scan_mem[:, o + CVR * E:o + (CVR + 1) * E]
        convb = scan_mem[:, o + (CVR + 1) * E:o + (CVR + 2) * E]
        place0 = cut(ffn_mem, 0, MH, 128)
        split0 = cut(ffn_mem, MH * 128, 4, 128)
        gf = cut(ffn_mem, 0, MF, N)
        pT = cut(ffn_mem, 0, 2 * H, L)
        g1 = cut(ffn_mem, 0, MM, N)
        ge = cut(ge_mem, 0, MM, N)
        cxT = cut(ge_mem, 0, MC, N)
        vaug = cut(ge_mem, MC * N, 4, H * VW)
        combT = ffn_mem[0:NEXP, MM * N:MM * N + N]

        P = ctx.enter_context(nc.psum_tensor("P", [128, 8, 512], F32))

        def V(name, i=0, rows=128):
            return vec[0:rows, VEC[name][0] + i:VEC[name][0] + i + 1]

        s_past = {n: signal("past_wait_" + n, 0) for n in ("pe", "dve", "pool")}
        s_cc, s_w = signal("conv_constants_in", 0), signal("weights_in", 0)
        s_setup, s_negA = signal("setup_done", 0), signal("negA_ready", 0)
        s_xp = [signal(f"patches_in_{r}", 16) for r in range(XPR)]
        s_cv = [signal(f"embedded_out_{r}", 32) for r in range(CVR)]
        s_text = signal("text_copied", 16)
        s_conv, e_conv = signal("conv_done", 0), signal("conv_evac", 0)
        s_h0 = signal("tokens_in", 32)
        s_row = [signal(f"rows_in_{r}", 32 * S // NROW) for r in range(NROW)]
        s_out = signal("out_written", 16 * NT)
        s_norm, s_tr, e_tr = norms("normalised", NT), norms("transposed", 2), norms("transposed_evac", 4)
        s_mv, s_sc = norms("moments", 1), norms("scales", 1)
        s_zg, s_tanh, e_z = signal("z_gate_done", 6), signal("z_tanh", 6), signal("z_evac", 6)
        s_xpj, e_xpj = signal("xproj_done", 2), signal("xproj_evac", 2)
        s_dtp, s_dtc, s_dtx = signal("dt_done", 6), signal("dt_clamped", 6), signal("dt_linear", 6)
        s_sp = signal("softplus_log", 1)
        s_acc0, s_rst = signal("acc_init", MD), signal("scan_reset", 1)
        s_u = signal("u_ready", 1)
        s_bc, s_ab = signal("bc_broadcast", S), signal("abar_ready", STEPS)
        s_bx, s_h, s_hc = signal("bx", STEPS), signal("h", STEPS), signal("hc", STEPS)
        s_add = signal("y_added", STEPS)
        s_wo, e_wo, s_x1 = signal("wout_done", 1), signal("wout_evac", NT), signal("x1_again", 1)
        s_h0w = signal("h0_plus_x2", 1)
        s_gu, s_tg, e_gu = signal("gate_up_done", 8), signal("ffn_tanh", 8), signal("gate_up_evac", 8)
        s_wd, e_wd = signal("down_done", NT), signal("down_evac", NT)
        s_qp, s_hi, s_lo = signal("qk_packed_done", 2 * MQ), signal("qk_upper", 2 * MQ), signal("qk_lower", 2 * MQ)
        s_qk, e_qk = signal("qk_done", 4 * MH), signal("qk_evac", 4 * MH)
        s_one, s_v, e_v = signal("vaug_ones", 1), signal("v_done", 8), signal("v_evac", 8)
        s_S, e_S, s_m2p = signal("scores_done", 4 * GB), signal("maxima", 4 * GB), signal("max_parts", GB)
        s_mt, e_mt = signal("maxT_done", GB), signal("maxT_evac", GB)
        s_nm, e_nm = signal("max_placed", GB), signal("max_added", GB)
        s_S2, e_S2 = signal("scoresT_done", 4 * GB), signal("exp_done", 4 * GB)
        s_cx, e_cx = signal("ctx_done", GB), signal("ctx_evac", GB)
        s_sum, s_ctx = signal("row_sums_spread", GB), signal("ctx_divided", GB)
        s_ow, e_ow, s_x5b = signal("attn_out_done", NT), signal("attn_out_evac", NT), signal("x5_plus_bias", NT)
        s_m1, e_m1 = signal("mlp1_done", 12), signal("mlp1_evac", 12)
        s_m2, e_m2 = signal("mlp2_done", NT), signal("mlp2_evac", NT)
        s_h1x = signal("h1_plus_x6", NT)
        s_lg, s_mx, s_ex = signal("logits_done", 1), signal("logits_shifted", 1), signal("gate_exp", 1)
        s_cmb, s_cbT, e_cbT = signal("comb_done", 1), signal("combT_done", 2), signal("combT_evac", 2)
        s_b2, e_b2 = signal("b2_done", NT), signal("b2_evac", NT)
        s_e1, e_e1 = signal("expert1_done", NU), signal("expert1_evac", NU)
        s_e2, e_e2 = signal("expert2_done", NEXP * NT), signal("expert2_evac", NEXP * NT)
        s_ew = [signal(f"expert_weights_in_{r}", 16 * NEXP // 2) for r in range(2)]
        c_dve_a, c_dve_b, c_act = signal("dve_chain_a", 3), signal("dve_chain_b", 29), signal("act_chain", 1)
        c_pool_a, c_pool_b = signal("pool_chain_a", 6), signal("pool_chain_b", 10)
        SETUP = 15
        BEGUN = first_phase(True, True, True)[1:]
        NPAIR = B // 2
        WOUT_AT = [(7, 0), (7, E), (6, 0), (6, E), (3, 0)]

        def hold(eng, name):
            eng.sem_inc(s_past[name].sem, 1)

        def padded(view):
            return view.rearrange("p (b l) -> p b l", b=GB)[:, :, 1:LP]

        def tok(view):
            return view.rearrange("p (b l) -> p b l", b=GB)

        def chunk(c):
            return slice(CH * c, CH * c + CH)

        def expert(ex):
            return cut(ew[:, ex % 2, :], 0, 2, HID), cut(ew[:, ex % 2, :], 2 * HID, MM, E)

        def q_or_k(u):
            c, m = divmod(u, 2 * MH)
            return c, m // MH, (qr, kr)[m // MH], m % MH

        block = ctx.enter_context(nc.Block())

        @block.sync
        def _(sp):
            def load_patches(p):
                if p >= XPR:
                    sp.wait_ge(s_conv.sem, p - XPR + 1)
                sp.dma_start(xp[:, p % XPR, :, :], dram["patches"][p, :, :, :]).then_inc(s_xp[p % XPR].sem, 16)

            for dst, n in ((cw, "cw"), (posb, "pos"), (convb, "cb")):
                sp.dma_start(dst, dram[n]).then_inc(s_cc.sem, 16)
            for p in range(XPR):
                load_patches(p)
            sp.dma_start(tokens[:, NP:L, :], dram["txt"]).then_inc(s_text.sem, 16)
            for dst, n in ((vec[:], "vec"), (mb2[:], "mb2"), (eb2[:], "eb2"), (ident[:], "ident"),
                           (earlier[:], "earlier"), (place0[0:2 * H], "place"), (split0, "split"),
                           (pick[:], "pick")):
                sp.dma_start(dst, dram[n]).then_inc(s_w.sem, 16)
            weights = list(ORDER)
            for p in range(NPAIR):
                if weights:
                    n = weights.pop(0)
                    sp.dma_start(W[n][:], dram[n]).then_inc(s_w.sem, 16)
                sp.wait_ge(e_conv.sem, p + 1)
                for q in range(2):
                    sp.dma_start(tokens[2 * p + q, 0:NP, :], cvs[NP * q:NP * q + NP, p % CVR, :]
                                 ).then_inc(s_cv[p % CVR].sem, 16)
                if p + XPR < NPAIR:
                    load_patches(p + XPR)
            for n in weights:
                sp.dma_start(W[n][:], dram[n]).then_inc(s_w.sem, 16)
            for r in range(CVR):
                sp.wait_ge(s_cv[r].sem, 32 * NPAIR // CVR)
            sp.wait_ge(s_text.sem, 16)
            flat = tokens.rearrange("(g b) l e -> g (b l) e", b=GB)
            whole = TILES[-1][0]

            def load(g, first):
                if not first:
                    sp.wait_ge(s_h0w.sem, s_h0w.at(g - 1))
                sp.dma_start(h0n[:, 0:NT - 1, :], flat[g, 0:whole, :].rearrange("(t p) e -> p t e", p=128)
                             ).then_inc(s_h0.sem, 16)
                sp.dma_start(h0n[0:N - whole, NT - 1, :], flat[g, whole:N, :]).then_inc(s_h0.sem, 16)

            def rows(g, states, first):
                for s in states:
                    if s == 0:
                        sp.wait_ge(e_xpj.sem, e_xpj.at(g))
                    if s >= NROW:
                        sp.wait_ge(s_bc.sem, s_bc.at(g, s - NROW + 1))
                    elif not first:
                        sp.wait_ge(s_bc.sem, s_bc.at(g - 1))
                    row = brows[32 * (s % NROW):32 * (s % NROW) + 1, :]
                    sp.dma_start(row[:, 0:N], xd[R + s:R + s + 1, :]).then_inc(s_row[s % NROW].sem, 16)
                    sp.dma_start(row[:, N:2 * N], xd[R + S + s:R + S + s + 1, :]).then_inc(s_row[s % NROW].sem, 16)

            def store(g):
                for t, (t0, nr) in enumerate(TILES):
                    sp.wait_ge(e_e2.sem, e_e2.at(g, (NEXP - 1) * NT + t + 1))
                    sp.dma_start(out[g, t0:t0 + nr, :], acc2[0:nr, t, :]).then_inc(s_out.sem, 16)

            def expert_weights(ex, used_by=None, outputs=0):
                if used_by is not None:
                    sp.wait_ge(s_e2.sem, s_e2.at(used_by, outputs))
                sp.dma_start(ew[:, ex % 2, :], dram["ew"][ex, :, :]).then_inc(s_ew[ex % 2].sem, 16)

            def group(g, first, e=None):
                load(g, first)
                rows(g, range(NROW), first)
                if e is None:
                    rows(g, range(NROW, S), first)
                    return
                expert_weights(2, e, NT)
                expert_weights(3, e, 2 * NT)
                rows(g, range(NROW, NROW + 2), first)
                expert_weights(0, e, 3 * NT)
                rows(g, range(NROW + 2, NROW + 4), first)
                store(e)
                expert_weights(1, e, 4 * NT)
                rows(g, range(NROW + 4, S), first)

            expert_weights(0)
            expert_weights(1)
            group(0, True)
            group(1, False)
            with sp.Fori(2, G) as g:
                group(g, False, g - 2)
            for ex in (2, 3):
                expert_weights(ex, G - 2, (ex - 1) * NT)
            store(G - 2)
            for ex in (0, 1):
                expert_weights(ex, G - 2, (ex + 3) * NT)
            for ex in (2, 3):
                expert_weights(ex, G - 1, (ex - 1) * NT)
            store(G - 1)
            sp.wait_ge(s_out.sem, s_out.at(G - 1))

        @block.tensor
        def _(pe):
            mm = nc.tensor.matmul

            def transposes(g, k, bank):
                for t, (t0, rows) in enumerate(TILES):
                    if k != 3:
                        pe.wait_ge(s_norm[k].sem, s_norm[k].at(g, t + 1))
                    src = xa if k in (3, 4) else hn
                    hold(pe, "pe")
                    bank0 = P[:, bank, t0:t0 + rows] if t < 4 else P[:, bank + 2, 0:rows]
                    bank1 = P[0:E1, bank + 1, t0:t0 + rows] if t < 4 else P[0:E1, bank + 2, 64:64 + rows]
                    nc.tensor.transpose(bank0, src[0:rows, t, 0:128], ident[0:rows, 0:rows])
                    last = nc.tensor.transpose(bank1, src[0:rows, t, 128:E], ident[0:rows, 0:rows])
                    if t in (3, 4):
                        last.then_inc(s_tr[k].sem, 1)

            def tile_out(g, t, lhs, rhs, done, freed, slabs, bank0=0):
                t0, rows = TILES[t]
                if t >= 4:
                    pe.wait_ge(freed.sem, freed.at(g, t - 3))
                for j, (kt, kr_) in enumerate(slabs):
                    last = mm(P[0:rows, bank0 + t % 4, 0:E], lhs[0:kr_, kt, t0:t0 + rows], rhs[0:kr_, kt, :],
                              start=(j == 0), stop=(j == len(slabs) - 1))
                last.then_inc(done.sem, 1)

            def k2(bank, w, m, c, src=hT, k1=E1):
                mm(bank, w[:, 0, 128 * m:128 * m + 128], src[:, 0, chunk(c)], start=True, stop=False)
                return mm(bank, w[0:k1, 1, 128 * m:128 * m + 128], src[0:k1, 1, chunk(c)], start=False, stop=True)

            def phase_one(a, b, e):
                for kind, k in first_phase(a is not None, b is not None, e is not None, 0)[0]:
                    if kind == "tr" and k == 0:
                        transposes(a, 0, 4)
                    elif kind == "tr":
                        if k == 1:
                            pe.wait_ge(e_wo.sem, e_wo.at(b))
                            if a is not None:
                                pe.wait_ge(s_dtc.sem, s_dtc.at(a))
                                pe.wait_ge(s_dtx.sem, s_dtx.at(a))
                        else:
                            pe.wait_ge(e_wd.sem, e_wd.at(b))
                        transposes(b, k, 4)
                    elif kind == "gu":
                        m, c = divmod(k, 2)
                        if k == 0:
                            pe.wait_ge(e_tr[1].sem, e_tr[1].at(b))
                        if k >= 2:
                            pe.wait_ge(e_gu.sem, e_gu.at(b, k - 1))
                        k2(P[:, 4 + 2 * (k % 2), 0:CH], W["wgf"], m, c)
                        k2(P[:, 5 + 2 * (k % 2), 0:CH], W["wup"], m, c).then_inc(s_gu.sem, 1)
                    elif kind == "dn":
                        if k == 0:
                            pe.wait_ge(e_gu.sem, e_gu.at(b))
                        tile_out(b, k, gf, W["wdn"], s_wd, e_wd, [(j, 128) for j in range(MF)], 4)
                    elif kind == "z":
                        m, c = divmod(k, 2)
                        if k == 0:
                            pe.wait_ge(e_tr[0].sem, e_tr[0].at(a))
                        if k >= 2:
                            pe.wait_ge(e_z.sem, e_z.at(a, k - 1))
                        k2(P[:, 4 + 2 * (k % 2), 0:CH], W["win"], m, c)
                        k2(P[:, 5 + 2 * (k % 2), 0:CH], W["wgate"], m, c).then_inc(s_zg.sem, 1)
                    elif kind == "xp":
                        if k == 0:
                            pe.wait_ge(e_z.sem, e_z.at(a))
                        for kt in range(MD):
                            last = mm(P[:, 4 + k, 0:CH], W["wxp"][:, kt, :], zu[:, kt, chunk(k)],
                                      start=(kt == 0), stop=(kt == MD - 1))
                        last.then_inc(s_xpj.sem, 1)
                    elif kind == "dt":
                        m, c = divmod(k, 2)
                        if k == 0:
                            pe.wait_ge(e_xpj.sem, e_xpj.at(a))
                        if k >= 4:
                            pe.wait_ge(s_dtc.sem, s_dtc.at(a, k - 3))
                            pe.wait_ge(s_dtx.sem, s_dtx.at(a, k - 3))
                        mm(P[:, 4 + k % 4, 0:CH], W["wdt"][0:R, 0, 128 * m:128 * m + 128], xd[0:R, chunk(c)],
                           start=True, stop=True).then_inc(s_dtp.sem, 1)
                    elif kind == "mm":
                        ex, r = divmod(k, UPE)
                        m, c = divmod(r, 2)
                        if k >= 2:
                            pe.wait_ge(e_e1.sem, e_e1.at(e, k - 1))
                        if r == 0:
                            pe.wait_ge(s_ew[ex % 2].sem, s_ew[ex % 2].at(e, 16 * (ex // 2 + 1)))
                        k2(P[:, k % 2, 0:CH], expert(ex)[0], m, c, xmT).then_inc(s_e1.sem, 1)
                    elif kind == "eout":
                        ex, t = divmod(k, NT)
                        t0, rows = TILES[t]
                        if t == 0:
                            pe.wait_ge(e_e1.sem, e_e1.at(e, UPE * ex + UPE))
                        if k >= 2:
                            pe.wait_ge(e_e2.sem, e_e2.at(e, k - 1))
                        for kt in range(MM):
                            last = mm(P[0:rows, 2 + k % 2, 0:E], ge[:, kt, t0:t0 + rows],
                                      expert(ex)[1][:, kt, :], start=(kt == 0), stop=(kt == MM - 1))
                        last.then_inc(s_e2.sem, 1)

            def unit_heads(hg):
                return [(a, 3 * hg + c, c) for c in range(MH // 2) for a in range(2)]

            def score_unit(g, kind, n):
                b, i = divmod(n, 4)
                x = 8 * b + 4 * kind + i
                if x >= 2:
                    pb, pr = divmod(x - 2, 8)
                    if pr < 4:
                        pe.wait_ge(e_S.sem, e_S.at(g, 4 * pb + pr + 1))
                    else:
                        pe.wait_ge(e_S2.sem, e_S2.at(g, 4 * pb + pr - 3))
                return 2 * (x % 2)

            def phase_two(b, s, begun=(0, 0)):
                for kind, k in second_phase(b is not None, s is not None, *begun):
                    if kind == "tr":
                        if k == 3:
                            pe.wait_ge(e_ow.sem, e_ow.at(b))
                        elif k == 4:
                            pe.wait_ge(e_m2.sem, e_m2.at(b))
                        transposes(b, k, 0)
                    elif kind == "qp":
                        c, m = divmod(k, MQ)
                        if k == 0:
                            pe.wait_ge(e_tr[2].sem, e_tr[2].at(b))
                        if k == MQ:
                            pe.wait_ge(s_ctx.sem, s_ctx.at(b, 1))
                            pe.wait_ge(e_nm.sem, e_nm.at(b, 2))
                        k2(P[:, 5 + m, 0:CH], W["wqk"], m, c, k1=E1 + 1).then_inc(s_qp.sem, 1)
                    elif kind == "qk":
                        c, is_k, _, _ = q_or_k(k)
                        u = k % (2 * MH)
                        if u <= 3:
                            pe.wait_ge(s_lo.sem, s_lo.at(b, MQ * c + (1, 1, 2, 3)[u]))
                        else:
                            pe.wait_ge(e_qk.sem, e_qk.at(b, k - 3))
                        r = slice(32 * (u % 4), 32 * (u % 4) + 32)
                        mm(P[:, 4 + k % 4, 0:CH], split[r, 2 * is_k, :], qk_hi[r, u // 4, :], start=True, stop=False)
                        mm(P[:, 4 + k % 4, 0:CH], split[r, 2 * is_k + 1, :], qk_lo[r, u // 4, :], start=False,
                           stop=True).then_inc(s_qk.sem, 1)
                    elif kind == "v":
                        sample, kh = divmod(k, 2)
                        k0, n = LH[kh]
                        cols = slice(sample * L + k0, sample * L + k0 + n)
                        if k % 4 == 0:
                            pe.wait_ge(e_qk.sem, e_qk.at(b, 2 * MH * (k // 4 + 1)))
                        if k % 4 >= 2:
                            pe.wait_ge(e_v.sem, e_v.at(b, k - 1))
                        mm(P[0:n, 6 + k % 2, 0:E], hT[:, 0, cols], W["wv"][:, 0, :], start=True, stop=False)
                        mm(P[0:n, 6 + k % 2, 0:E], hT[0:E1 + 1, 1, cols], W["wv"][0:E1 + 1, 1, :],
                           start=False, stop=True).then_inc(s_v.sem, 1)
                    elif kind == "S":
                        sample, i = divmod(k, 4)
                        q, hg = divmod(i, 2)
                        q0, n = LH[q]
                        if i == 0:
                            pe.wait_ge(e_qk.sem, e_qk.at(b, 2 * MH * (sample // 2 + 1)))
                        bank = score_unit(b, 0, k)
                        for a, m, c in unit_heads(hg):
                            r = slice(HP * a, HP * a + HP)
                            last = mm(P[0:n, bank + a, LE * c:LE * c + LE], qr[r, m, sample % 2, q0:q0 + n],
                                      kr[r, m, sample % 2, :], start=True, stop=True)
                        last.then_inc(s_S.sem, 1)
                    elif kind == "nm":
                        pe.wait_ge(s_m2p.sem, s_m2p.at(b, k + 1))
                        if k >= 2:
                            pe.wait_ge(s_ctx.sem, s_ctx.at(b, 2))
                        for q, (q0, n) in enumerate(LH):
                            hold(pe, "pe")
                            last = nc.tensor.transpose(P[0:2 * H, 4, q0:q0 + n],
                                                       mneg[0:n, q, :, :].rearrange("p a b -> p (a b)"),
                                                       ident[0:n, 0:n])
                        last.then_inc(s_mt.sem, 1)
                        pe.wait_ge(e_mt.sem, e_mt.at(b, k + 1))
                        if k % 2 == 0:
                            pe.wait_ge(e_v.sem, e_v.at(b, 4 * (k // 2 + 1)))
                        if k:
                            pe.wait_ge(e_nm.sem, e_nm.at(b, k))
                        for m in range(MH):
                            last = mm(P[:, 6 + m // 3, LE * (m % 3):LE * (m % 3) + LE], place[:, m, :], mT[:, :],
                                      start=True, stop=True)
                        last.then_inc(s_nm.sem, 1)
                    elif kind == "S2":
                        sample, i = divmod(k, 4)
                        kh, hg = divmod(i, 2)
                        k0, n = LH[kh]
                        if i == 0:
                            pe.wait_ge(e_nm.sem, e_nm.at(b, sample + 1))
                        bank = score_unit(b, 1, k)
                        for a, m, c in unit_heads(hg):
                            r = slice(HP * a, HP * a + HP)
                            last = mm(P[0:n, bank + a, LE * c:LE * c + LE], kr[r, m, sample % 2, k0:k0 + n],
                                      qr[r, m, sample % 2, :], start=True, stop=True)
                        last.then_inc(s_S2.sem, 1)
                    elif kind == "ctx":
                        if k == 0:
                            pe.wait_ge(s_one.sem, s_one.at(b))
                        else:
                            pe.wait_ge(e_cx.sem, e_cx.at(b, k))
                        if k == 1:
                            pe.wait_ge(e_qk.sem, e_qk.at(b))
                        if k % 2 == 0:
                            pe.wait_ge(e_v.sem, e_v.at(b, 4 * (k // 2 + 1)))
                        pe.wait_ge(e_S2.sem, e_S2.at(b, 4 * k + 4))
                        for h in range(H):
                            m, a = divmod(h, 2)
                            at = (m // 3) * 6 + a * 3 + m % 3
                            slab, r = divmod(h * VW, 128)
                            for kh, (_, kn) in enumerate(LH):
                                last = mm(P[r:r + VW, 5, L * slab:L * slab + L],
                                          vaug[0:kn, 2 * (k % 2) + kh, VW * h:VW * h + VW],
                                          pT[0:kn, kh * H + at, :], start=(kh == 0), stop=(kh == 1))
                        last.then_inc(s_cx.sem, 1)
                    elif kind == "sum":
                        pe.wait_ge(e_cx.sem, e_cx.at(b, k + 1))
                        mm(P[:, 4, 0:MC * L], pick[:, :], cs[:, :, :].rearrange("p a l -> p (a l)"), start=True,
                           stop=True).then_inc(s_sum.sem, 1)
                    elif kind == "ow":
                        if k == 0:
                            pe.wait_ge(s_ctx.sem, s_ctx.at(b))
                        tile_out(b, k, cxT, W["wo"], s_ow, e_ow, [(j, 128) for j in range(MC)])
                    elif kind == "m1":
                        m, c = divmod(k, 2)
                        if k == 0:
                            pe.wait_ge(e_tr[3].sem, e_tr[3].at(b))
                        if k >= 4:
                            pe.wait_ge(e_m1.sem, e_m1.at(b, k - 3))
                        k2(P[:, 4 + k % 4, 0:CH], W["mw1"], m, c).then_inc(s_m1.sem, 1)
                    elif kind == "m2":
                        if k == 0:
                            pe.wait_ge(e_m1.sem, e_m1.at(b))
                        tile_out(b, k, g1, W["mw2"], s_m2, e_m2, [(j, 128) for j in range(MM)])
                    elif kind == "wout":
                        pe.wait_ge(s_add.sem, s_add.at(s))
                        if b is not None:
                            pe.wait_ge(e_m2.sem, e_m2.at(b, 4))
                        for (t0, rows), (bank, col) in zip(TILES, WOUT_AT):
                            for kt in range(MD):
                                last = mm(P[0:rows, bank, col:col + E], acc[:, kt, t0:t0 + rows], W["wout"][:, kt, :],
                                          start=(kt == 0), stop=(kt == MD - 1))
                        last.then_inc(s_wo.sem, 1)
                    elif kind == "gate":
                        pe.wait_ge(e_tr[4].sem, e_tr[4].at(b))
                        for t, (t0, rows) in enumerate(TILES):
                            dst = P[0:rows, 4, NEXP * t:NEXP * t + NEXP]
                            mm(dst, xmT[:, 0, t0:t0 + rows], W["gw"][:, 0, :], start=True, stop=False)
                            last = mm(dst, xmT[0:E1 + 1, 1, t0:t0 + rows], W["gw"][0:E1 + 1, 1, :],
                                      start=False, stop=True)
                        last.then_inc(s_lg.sem, 1)
                        pe.wait_ge(s_cmb.sem, s_cmb.at(b))
                        for t, (t0, rows) in enumerate(TILES):
                            dst = P[0:NEXP, 5, t0:t0 + rows] if t < 4 else P[0:NEXP, 4, 64:64 + rows]
                            last = nc.tensor.transpose(dst, comb[0:rows, t, :], ident[0:rows, 0:rows])
                            if t in (3, 4):
                                last.then_inc(s_cbT.sem, 1)
                    elif kind == "b2":
                        t0, rows = TILES[k]
                        if k == 0:
                            pe.wait_ge(e_cbT.sem, e_cbT.at(b))
                        if k >= 3:
                            pe.wait_ge(e_b2.sem, e_b2.at(b, k - 2))
                        mm(P[0:rows, k % 3, 0:E], combT[:, t0:t0 + rows], eb2[:, :], start=True,
                           stop=True).then_inc(s_b2.sem, 1)

            pe.wait_ge(s_cc.sem, 48)
            for p in range(NPAIR):
                pe.wait_ge(s_xp[p % XPR].sem, 16 * (p // XPR + 1))
                if p >= 4:
                    pe.wait_ge(e_conv.sem, p - 3)
                for kt in range(KC):
                    last = mm(P[:, p % 4, 0:E], xp[:, p % XPR, kt, :], cw[:, kt, :],
                              start=(kt == 0), stop=(kt == KC - 1))
                last.then_inc(s_conv.sem, 1)
            pe.wait_ge(s_w.sem, 16 * (len(ORDER) + 8))
            pe.wait_ge(s_setup.sem, SETUP)
            pe.wait_ge(e_conv.sem, NPAIR)
            phase_one(0, None, None)
            phase_two(None, 0)
            pe.wait_ge(e_wo.sem, e_wo.at(0))
            phase_one(1, 0, None)
            pe.wait_ge(s_dtc.sem, s_dtc.at(1))
            pe.wait_ge(s_dtx.sem, s_dtx.at(1))
            phase_two(0, 1)
            pe.wait_ge(e_b2.sem, e_b2.at(0))
            with pe.Fori(2, G) as g:
                pe.wait_ge(e_wo.sem, e_wo.at(g - 1))
                phase_one(g, g - 1, g - 2)
                pe.wait_ge(e_e2.sem, e_e2.at(g - 2))
                phase_two(g - 1, g, BEGUN)
                pe.wait_ge(e_b2.sem, e_b2.at(g - 1))
            pe.wait_ge(e_wo.sem, e_wo.at(G - 1))
            phase_one(None, G - 1, G - 2)
            pe.wait_ge(e_e2.sem, e_e2.at(G - 2))
            phase_two(G - 1, None)
            pe.wait_ge(e_b2.sem, e_b2.at(G - 1))
            phase_one(None, None, G - 1)

        @block.scalar
        def _(act):
            chain = Chain(c_act, act)

            def A(out_, in_, func, **k):
                return nc.scalar.activation(out_, in_, func, **k)

            def evac_transposed(g, k, bank, dst, scale=None, bias=None):
                parts = [(0, P[:, bank, 0:512], dst[:, 0, 0:512], 0, 128),
                         (0, P[0:E1, bank + 1, 0:512], dst[0:E1, 1, 0:512], 1, E1),
                         (1, P[:, bank + 2, 0:N - 512], dst[:, 0, 512:N], 0, 128),
                         (1, P[0:E1, bank + 2, 64:64 + N - 512], dst[0:E1, 1, 512:N], 1, E1)]
                for late, src, d, slab, rows in parts:
                    act.wait_ge(s_tr[k].sem, s_tr[k].at(g, 1 + late))
                    kw = {}
                    if scale:
                        kw["scale"] = V(scale, slab, rows)
                    if bias:
                        kw["bias"] = V(bias, slab, rows)
                    A(d, src, ACT.Identity, **kw).then_inc(e_tr[k].sem, 1)

            def decay(g, k):
                state, m = divmod(k, MD)
                if k == 0:
                    act.wait_ge(s_rst.sem, s_rst.at(g))
                if k >= NABAR:
                    act.wait_ge(s_h.sem, s_h.at(g, k - NABAR + 1))
                A(padded(abar[:, k % NABAR, :]), tok(dt[:, m, :]), ACT.Exp,
                  scale=negA[:, m * S + state:m * S + state + 1]).then_inc(s_ab.sem, 1)

            def phase_one(a, b, e):
                for kind, k in first_phase(a is not None, b is not None, e is not None)[0]:
                    if kind == "tr" and k == 0:
                        chain.begin(a)
                        evac_transposed(a, 0, 4, hT, "w1n")
                    elif kind == "tr":
                        evac_transposed(b, k, 4, hT, *(("wfn",), ("g1", "b1"))[k - 1])
                    elif kind == "gu":
                        m, c = divmod(k, 2)
                        act.wait_ge(s_gu.sem, s_gu.at(b, k + 1))
                        A(gf[:, m, chunk(c)], P[:, 4 + 2 * (k % 2), 0:CH], ACT.Tanh, scale=0.5
                          ).then_inc(s_tg.sem, 1)
                    elif kind == "z":
                        m, c = divmod(k, 2)
                        act.wait_ge(s_zg.sem, s_zg.at(a, k + 1))
                        A(zu[:, m, chunk(c)], P[:, 5 + 2 * (k % 2), 0:CH], ACT.Tanh, scale=0.5
                          ).then_inc(s_tanh.sem, 1)
                    elif kind == "xp":
                        act.wait_ge(s_xpj.sem, s_xpj.at(a, k + 1))
                        A(xd[:, chunk(k)], P[:, 4 + k, 0:CH], ACT.Copy).then_inc(e_xpj.sem, 1)
                    elif kind == "dt":
                        m, c = divmod(k, 2)
                        act.wait_ge(s_dtp.sem, s_dtp.at(a, k + 1))
                        act.wait_ge(s_dtc.sem, s_dtc.at(a, k + 1))
                        A(dt[:, m, chunk(c)], P[:, 4 + k % 4, 0:CH], ACT.Identity, bias=V("bdt", m)
                          ).then_inc(s_dtx.sem, 1)
                    elif kind == "dtend":
                        chain.link(A(cl[:, :, :], cl[:, :, :], ACT.Exp))
                        A(cl[:, :, :], cl[:, :, :], ACT.Ln, bias=1.0).then_inc(s_sp.sem, 1)
                        chain.end()
                    elif kind == "dec":
                        decay(a, k)
                    elif kind == "act":
                        ex, r = divmod(k, UPE)
                        m, c = divmod(r, 2)
                        act.wait_ge(s_e1.sem, s_e1.at(e, k + 1))
                        if ex and r == 0:
                            act.wait_ge(s_e2.sem, s_e2.at(e, ex * NT))
                        A(ge[:, m, chunk(c)], P[:, k % 2, 0:CH], ACT.Gelu, bias=V("eb1", ex * MM + m)
                          ).then_inc(e_e1.sem, 1)

            def phase_two(b, s, begun=(0, 0)):
                for kind, k in second_phase(b is not None, s is not None, *begun):
                    if kind == "dec":
                        decay(s, k)
                    elif kind == "tr":
                        evac_transposed(b, k, 0, *((hT,), (xmT, "g2", "b2"))[k - 3])
                    elif kind == "qp":
                        act.wait_ge(s_qp.sem, s_qp.at(b, k + 1))
                        A(qk_hi[:, k % MQ, :], P[:, 5 + k % MQ, 0:CH], ACT.Identity).then_inc(s_hi.sem, 1)
                    elif kind == "qk":
                        c, is_k, dst, m = q_or_k(k)
                        act.wait_ge(s_qk.sem, s_qk.at(b, k + 1))
                        if k == 2 * MH:
                            act.wait_ge(s_S2.sem, s_S2.at(b, 8))
                        kw = {"bias": V("kone")} if is_k else {}
                        A(dst[:, m, :, 0:L], P[:, 4 + k % 4, 0:CH].rearrange("p (s l) -> p s l", s=2), ACT.Identity,
                          **kw).then_inc(e_qk.sem, 1)
                    elif kind == "v":
                        n = LH[k % 2][1]
                        act.wait_ge(s_v.sem, s_v.at(b, k + 1))
                        if k == 0:
                            act.wait_ge(s_one.sem, s_one.at(b))
                        if k == 4:
                            act.wait_ge(s_cx.sem, s_cx.at(b, 2))
                        A(vaug[0:n, k % 4, :].rearrange("p (h w) -> p h w", w=VW)[:, :, 0:HD],
                          P[0:n, 6 + k % 2, 0:E].rearrange("p (h w) -> p h w", w=HD), ACT.Copy
                          ).then_inc(e_v.sem, 1)
                    elif kind == "nm":
                        act.wait_ge(s_mt.sem, s_mt.at(b, k + 1))
                        A(mT[:, 0:L], P[0:2 * H, 4, 0:L], ACT.Copy).then_inc(e_mt.sem, 1)
                    elif kind == "S2":
                        sample, i = divmod(k, 4)
                        kh, hg = divmod(i, 2)
                        bank = 2 * ((8 * sample + 4 + i) % 2)
                        n = LH[kh][1]
                        act.wait_ge(s_S2.sem, s_S2.at(b, k + 1))
                        if sample and i == 0:
                            act.wait_ge(s_cx.sem, s_cx.at(b, sample))
                        dst = pT[0:n, kh * H + 6 * hg:kh * H + 6 * hg + 6, :].rearrange("p (a c) l -> p a c l", a=2)
                        src = P[0:n, bank:bank + 2, 0:3 * LE].rearrange("p a (c l) -> p a c l", l=LE)
                        A(dst, src[:, :, :, 0:L], ACT.Exp).then_inc(e_S2.sem, 1)
                    elif kind == "ctx":
                        act.wait_ge(s_cx.sem, s_cx.at(b, k + 1))
                        if k:
                            act.wait_ge(s_ctx.sem, s_ctx.at(b, k))
                        A(cs[:, :, :].rearrange("p a l -> p (a l)"), P[:, 5, 0:MC * L], ACT.Copy
                          ).then_inc(e_cx.sem, 1)
                    elif kind == "m1":
                        m, c = divmod(k, 2)
                        act.wait_ge(s_m1.sem, s_m1.at(b, k + 1))
                        A(g1[:, m, chunk(c)], P[:, 4 + k % 4, 0:CH], ACT.Gelu, bias=V("mb1", m)
                          ).then_inc(e_m1.sem, 1)
                    elif kind == "gate":
                        act.wait_ge(s_mx.sem, s_mx.at(b))
                        A(gs[:, 2, :], gs[:, 1, :], ACT.Exp).then_inc(s_ex.sem, 1)

            act.wait_ge(s_w.sem, 16 * (len(ORDER) + 8))
            A(negA[:], vec[:, VEC["alog"][0]:VEC["alog"][0] + MD * S], ACT.Exp).then_inc(s_negA.sem, 1)
            act.wait_ge(s_negA.sem, 2)
            act.wait_ge(s_setup.sem, SETUP)
            phase_one(0, None, None)
            phase_two(None, 0)
            phase_one(1, 0, None)
            phase_two(0, 1)
            with act.Fori(2, G) as g:
                phase_one(g, g - 1, g - 2)
                phase_two(g - 1, g, BEGUN)
            phase_one(None, G - 1, G - 2)
            phase_two(G - 1, None)
            phase_one(None, None, G - 1)

        @block.vector
        def _(dve):
            T = nc.vector
            chain_a, chain_b = Chain(c_dve_a, dve), Chain(c_dve_b, dve)

            def moments(src, g, k, chain):
                mv = mvs[k > 0]
                for t, (t0, rows) in enumerate(TILES):
                    ins = T.bn_stats(stats[0:rows, t, :], src[0:rows, t, :])
                chain.link(ins)
                hold(dve, "dve")
                for t, (t0, rows) in enumerate(TILES):
                    ins = T.bn_aggr(mv[0:rows, t, :], stats[0:rows, t, :])
                ins.then_inc(s_mv[k].sem, 1)
                dve.wait_ge(s_sc[k].sem, s_sc[k].at(g))

            def scaled(dst, src, k, col, t, centre=True):
                rows = TILES[t][1]
                s = sms[k > 0][0:rows, col, t:t + 1]
                if centre:
                    return T.tensor_scalar(dst[0:rows, t, :], src[0:rows, t, :], mvs[k > 0][0:rows, t, 0:1], s,
                                           ALU.subtract, ALU.mult)
                return T.tensor_scalar(dst[0:rows, t, :], src[0:rows, t, :], s, None, ALU.mult)

            def plus_psum(g, t, dst, done, evac, bank0=0, banks=4):
                rows = TILES[t][1]
                dve.wait_ge(done.sem, done.at(g, t + 1))
                T.tensor_tensor(dst[0:rows, t, :], dst[0:rows, t, :], P[0:rows, bank0 + t % banks, 0:E], ALU.add
                                ).then_inc(evac.sem, 1)

            def bx(g, j):
                s, m = divmod(j, MD)
                if j == 0:
                    dve.wait_ge(s_rst.sem, s_rst.at(g))
                    dve.wait_ge(s_u.sem, s_u.at(g))
                if m == 0:
                    dve.wait_ge(s_bc.sem, s_bc.at(g, s + 1))
                if j >= NRING:
                    dve.wait_ge(s_add.sem, s_add.at(g, j - NRING + 1))
                T.tensor_tensor(padded(ring[:, j % NRING, :]), tok(zu[:, m, :]), tok(bc[:, s % NBC, 0:N]),
                                ALU.mult).then_inc(s_bx.sem, 1)

            def scan(g, j):
                dve.wait_ge(s_bx.sem, s_bx.at(g, j + 1))
                dve.wait_ge(s_ab.sem, s_ab.at(g, j + 1))
                v = ring[:, j % NRING, :]
                T.tensor_tensor_scan(v, abar[:, j % NABAR, :], v, 0.0, ALU.mult, ALU.add).then_inc(s_h.sem, 1)

            def hc(g, j):
                s, m = divmod(j, MD)
                dve.wait_ge(s_h.sem, s_h.at(g, j + 1))
                v = padded(ring[:, j % NRING, :])
                T.tensor_tensor(v, v, tok(bc[:, s % NBC, N:2 * N]), ALU.mult).then_inc(s_hc.sem, 1)

            def scan_step(g, k):
                if k < STEPS:
                    bx(g, k)
                if 1 <= k <= STEPS:
                    scan(g, k - 1)
                if k >= 2:
                    hc(g, k - 2)

            def phase_one(a, b, e):
                link = chain_b.link
                if b is not None:
                    chain_b.begin(b)
                for kind, k in first_phase(a is not None, b is not None, e is not None)[0]:
                    if kind == "norm" and k == 0:
                        chain_a.begin(a)
                        dve.wait_ge(s_h0.sem, s_h0.at(a))
                        moments(h0n, a, 0, chain_a)
                        for t in range(NT):
                            scaled(hn, h0n, 0, 6, t).then_inc(s_norm[0].sem, 1)
                    elif kind == "norm" and k == 1:
                        moments(xa, b, 1, chain_b)
                        for t in range(NT):
                            scaled(hn, xa, 1, 2, t, centre=False).then_inc(s_norm[1].sem, 1)
                    elif kind == "norm" and k == 2:
                        dve.wait_ge(e_wd.sem, e_wd.at(b))
                        moments(h0, b, 2, chain_b)
                        for t in range(NT):
                            scaled(hn, h0, 2, 6, t).then_inc(s_norm[2].sem, 1)
                        for t in range(NT):
                            ins = scaled(xa, h0, 2, 2, t)
                        link(ins)
                    elif kind == "gu":
                        m, c = divmod(k, 2)
                        dve.wait_ge(s_tg.sem, s_tg.at(b, k + 1))
                        v = gf[:, m, chunk(c)]
                        link(T.scalar_tensor_tensor(out=v, in0=v, scalar=1.0, in1=P[:, 4 + 2 * (k % 2), 0:CH],
                                                    op0=ALU.add, op1=ALU.mult))
                        T.tensor_tensor(v, v, P[:, 5 + 2 * (k % 2), 0:CH], ALU.mult).then_inc(e_gu.sem, 1)
                    elif kind == "dn":
                        if k == 0:
                            dve.wait_ge(s_h0w.sem, s_h0w.at(b))
                        plus_psum(b, k, h0, s_wd, e_wd, 4)
                    elif kind == "z":
                        m, c = divmod(k, 2)
                        dve.wait_ge(s_tanh.sem, s_tanh.at(a, k + 1))
                        v = zu[:, m, chunk(c)]
                        T.scalar_tensor_tensor(out=v, in0=v, scalar=1.0, in1=P[:, 4 + 2 * (k % 2), 0:CH],
                                               op0=ALU.add, op1=ALU.mult).then_inc(e_z.sem, 1)
                    elif kind == "dt":
                        m, c = divmod(k, 2)
                        dve.wait_ge(s_dtp.sem, s_dtp.at(a, k + 1))
                        T.tensor_scalar(cl[:, m, chunk(c)], P[:, 4 + k % 4, 0:CH], V("bdt", m), SPC,
                                        ALU.add, ALU.min).then_inc(s_dtc.sem, 1)
                    elif kind == "dtend":
                        dve.wait_ge(s_sp.sem, s_sp.at(a))
                        dve.wait_ge(s_dtx.sem, s_dtx.at(a))
                        chain_a.link(T.tensor_tensor(dt[:, :, :], dt[:, :, :], cl[:, :, :], ALU.max))
                        for m in range(MD):
                            T.tensor_scalar(acc[:, m, :], zu[:, m, :], V("dsk", m), None, ALU.mult
                                            ).then_inc(s_acc0.sem, 1)
                        chain_a.link(T.memset(abar[:, :, :].rearrange("p a (b l) -> p a b l", l=LP)[:, :, :, 0:1], 0.0))
                        T.memset(ring[:, :, :].rearrange("p a (b l) -> p a b l", l=LP)[:, :, :, 0:1], 0.0
                                 ).then_inc(s_rst.sem, 1)
                        dve.wait_ge(s_acc0.sem, s_acc0.at(a))
                        T.tensor_tensor(zu[:, :, :], zu[:, :, :], dt[:, :, :], ALU.mult).then_inc(s_u.sem, 1)
                        chain_a.end()
                    elif kind == "scn":
                        scan_step(a, k)
                    elif kind == "eout":
                        ex, t = divmod(k, NT)
                        rows = TILES[t][1]
                        dve.wait_ge(s_e2.sem, s_e2.at(e, k + 1))
                        if ex:
                            dve.wait_ge(e_e2.sem, e_e2.at(e, k - NT + 1))
                        else:
                            dve.wait_ge(e_b2.sem, e_b2.at(e))
                        T.scalar_tensor_tensor(out=acc2[0:rows, t, :], in0=P[0:rows, 2 + k % 2, 0:E],
                                               scalar=comb[0:rows, t, ex:ex + 1], in1=acc2[0:rows, t, :],
                                               op0=ALU.mult, op1=ALU.add).then_inc(e_e2.sem, 1)

            def gates(g):
                link = chain_b.link
                dve.wait_ge(s_lg.sem, s_lg.at(g))
                rl = TILES[-1][1]
                T.tensor_copy(gs[:, 0, 0:4 * NEXP], P[:, 4, 0:4 * NEXP])
                link(T.tensor_copy(gs[0:rl, 0, 4 * NEXP:NT * NEXP], P[0:rl, 4, 4 * NEXP:NT * NEXP]))

                def per_token(v):
                    return v.rearrange("p (t e) -> p t e", t=NT)

                def spread(v):
                    return v.unsqueeze(2).to_broadcast([128, NT, NEXP])

                l3 = per_token(gs[:, 0, :])
                link(T.tensor_reduce(gm[:, 0, :], l3, AX.X, ALU.max))
                T.tensor_tensor(per_token(gs[:, 1, :]), l3, spread(gm[:, 0, :]), ALU.subtract
                                ).then_inc(s_mx.sem, 1)
                for x in range(NEXP):
                    lx = l3[:, :, x:x + 1].to_broadcast([128, NT, NEXP])
                    cols = slice(NEXP * x, NEXP * x + NEXP)
                    T.tensor_tensor(gr[:, 0, :, cols], l3, lx, ALU.is_gt)
                    ins = T.tensor_tensor(gr[:, 1, :, cols], l3, lx, ALU.is_equal)
                link(ins)
                link(T.tensor_tensor(gr[:, 1, :, :], gr[:, 1, :, :],
                                     earlier[:, :, :].rearrange("p e j -> p (e j)").unsqueeze(1).to_broadcast(
                                         [128, NT, NEXP * NEXP]), ALU.mult))
                link(T.tensor_tensor(gr[:, 0, :, :], gr[:, 0, :, :], gr[:, 1, :, :], ALU.add))
                link(T.tensor_reduce(per_token(gs[:, 3, :]),
                                     gr[:, 0, :, :].rearrange("p t (e j) -> p t e j", e=NEXP), AX.X, ALU.add))
                dve.wait_ge(s_ex.sem, s_ex.at(g))
                link(T.scalar_tensor_tensor(out=gs[:, 4, :], in0=gs[:, 3, :], scalar=1.5, in1=gs[:, 2, :],
                                            op0=ALU.is_lt, op1=ALU.mult))
                link(T.tensor_reduce(gm[:, 1, :], per_token(gs[:, 4, :]), AX.X, ALU.add))
                link(T.reciprocal(gm[:, 2, :], gm[:, 1, :]))
                T.tensor_tensor(comb[:, :, :], per_token(gs[:, 4, :]), spread(gm[:, 2, :]), ALU.mult
                                ).then_inc(s_cmb.sem, 1)
                dve.wait_ge(s_cbT.sem, s_cbT.at(g, 1))
                T.tensor_copy(combT[:, 0:512], P[0:NEXP, 5, 0:512]).then_inc(e_cbT.sem, 1)
                dve.wait_ge(s_cbT.sem, s_cbT.at(g, 2))
                T.tensor_copy(combT[:, 512:N], P[0:NEXP, 4, 64:64 + N - 512]).then_inc(e_cbT.sem, 1)

            def phase_two(b, s, begun=(0, 0)):
                link = chain_b.link
                for kind, k in second_phase(b is not None, s is not None, *begun):
                    if kind == "scn":
                        scan_step(s, k)
                    elif kind == "norm" and k == 3:
                        dve.wait_ge(e_m2.sem, e_m2.at(b))
                        moments(hn, b, 3, chain_b)
                        for t in range(NT):
                            scaled(xa, hn, 3, 2, t).then_inc(s_norm[4].sem, 1)
                    elif kind == "qp":
                        dve.wait_ge(s_hi.sem, s_hi.at(b, k + 1))
                        T.tensor_tensor(qk_lo[:, k % MQ, :], P[:, 5 + k % MQ, 0:CH],
                                        qk_hi[:, k % MQ, :].bitcast(F32), ALU.subtract).then_inc(s_lo.sem, 1)
                    elif kind == "v" and k == 0:
                        T.memset(vaug[:, :, :].rearrange("p a (h w) -> p a h w", w=VW)[:, :, :, HD:VW], 1.0
                                 ).then_inc(s_one.sem, 1)
                    elif kind == "S":
                        sample, i = divmod(k, 4)
                        q, hg = divmod(i, 2)
                        n = LH[q][1]
                        bank = 2 * ((8 * sample + i) % 2)
                        dve.wait_ge(s_S.sem, s_S.at(b, k + 1))
                        dst = mf[0:n, q, :].rearrange("p (m a) -> p a m", a=2)[:, :, 3 * hg:3 * hg + 3]
                        src = P[0:n, bank:bank + 2, 0:3 * LE].rearrange("p a (c l) -> p a c l", l=LE)[:, :, :, 0:L]
                        T.tensor_reduce(dst, src, AX.X, ALU.max, negate=True).then_inc(e_S.sem, 1)
                        if i == 3:
                            dve.wait_ge(e_S.sem, e_S.at(b, 4 * sample + 4))
                            if sample:
                                dve.wait_ge(s_mt.sem, s_mt.at(b, sample))
                            link(T.tensor_copy(mneg[:, :, 0, :].bitcast(F32R), mf[:, :, :]))
                            T.tensor_tensor(mneg[:, :, 1, :].bitcast(F32R), mf[:, :, :], mneg[:, :, 0, :],
                                            ALU.subtract).then_inc(s_m2p.sem, 1)
                    elif kind == "nm":
                        dve.wait_ge(s_nm.sem, s_nm.at(b, k + 1))
                        v = qr[:, :, k % 2, 0:L].rearrange("p (h m) l -> p h m l", h=2)
                        T.tensor_tensor(v, v.bitcast(F32),
                                        P[:, 6:8, 0:3 * LE].rearrange("p h (m l) -> p h m l", l=LE)[:, :, :, 0:L],
                                        ALU.add).then_inc(e_nm.sem, 1)
                    elif kind == "sum":
                        dve.wait_ge(s_sum.sem, s_sum.at(b, k + 1))
                        v = cxT[:, :, L * k:L * k + L]
                        link(T.reciprocal(v, P[:, 4, 0:MC * L].rearrange("p (a l) -> p a l", l=L)))
                        T.tensor_tensor(v, v, cs[:, :, :], ALU.mult).then_inc(s_ctx.sem, 1)
                    elif kind == "ow":
                        plus_psum(b, k, xa, s_ow, e_ow)
                    elif kind == "m2":
                        if k == 0:
                            dve.wait_ge(s_x5b.sem, s_x5b.at(b))
                        plus_psum(b, k, hn, s_m2, e_m2)
                    elif kind == "gate":
                        gates(b)
                    elif kind == "b2":
                        if k == 0:
                            dve.wait_ge(s_h1x.sem, s_h1x.at(b))
                        plus_psum(b, k, acc2, s_b2, e_b2, banks=3)
                if b is not None:
                    chain_b.end()

            def project(g, after_b):
                if after_b is not None:
                    dve.wait_ge(s_x5b.sem, s_x5b.at(after_b))
                for t in range(NT):
                    ins = scaled(xa, h0n, 0, 2, t)
                ins.then_inc(s_x1.sem, 1)
                dve.wait_ge(s_x1.sem, s_x1.at(g))
                dve.wait_ge(s_wo.sem, s_wo.at(g))
                for t, ((_, rows), (bank, col)) in enumerate(zip(TILES, WOUT_AT)):
                    T.tensor_tensor(xa[0:rows, t, :], xa[0:rows, t, :], P[0:rows, bank, col:col + E], ALU.add
                                    ).then_inc(e_wo.sem, 1)
                dve.wait_ge(e_wo.sem, e_wo.at(g))
                for t, (t0, rows) in enumerate(TILES):
                    ins = T.tensor_tensor(h0[0:rows, t, :], h0n[0:rows, t, :], xa[0:rows, t, :], ALU.add)
                ins.then_inc(s_h0w.sem, 1)

            dve.wait_ge(s_cc.sem, 48)
            T.tensor_tensor(posb, posb, convb, ALU.add).then_inc(s_setup.sem, 1)
            dve.wait_ge(s_setup.sem, 1)
            for p in range(NPAIR):
                dve.wait_ge(s_conv.sem, p + 1)
                if p >= CVR:
                    dve.wait_ge(s_cv[p % CVR].sem, 32 * (p // CVR))
                T.tensor_tensor(cvs[:, p % CVR, :], P[:, p % 4, 0:E], posb, ALU.add).then_inc(e_conv.sem, 1)
            dve.wait_ge(s_w.sem, 16 * (len(ORDER) + 8))
            for ins in (T.tensor_scalar(W["win"][:], W["win"][:], 0.5, None, ALU.mult),
                        T.tensor_scalar(W["wup"][:], W["wup"][:], 0.5, None, ALU.mult),
                        T.tensor_scalar(W["wqk"][:, :, 0:E], W["wqk"][:, :, 0:E], HD ** -0.5, None, ALU.mult),
                        T.tensor_copy(place[:], place0[0:2 * H]), T.tensor_copy(split[:], split0),
                        T.memset(hT[E1:128, 1, :], 1.0), T.memset(xmT[E1:128, 1, :], 1.0),
                        T.memset(qr[:, :, :, L:LE].bitcast(F32), 0.0), T.memset(kr[:, :, :, L:LE].bitcast(F32), 0.0),
                        T.memset(mT[:, L:LE].bitcast(F32), 0.0), T.memset(gs[:], 0.0), T.memset(comb[:], 0.0),
                        T.memset(mf[:], 0.0), T.memset(half[:], -0.5)):
                ins.then_inc(s_setup.sem, 1)
            for mv in mvs:
                T.memset(mv[:], 1.0)
            dve.wait_ge(s_negA.sem, 1)
            T.tensor_scalar(negA[:], negA[:], -1.0, None, ALU.mult).then_inc(s_negA.sem, 1)
            dve.wait_ge(s_setup.sem, SETUP)
            dve.wait_ge(s_negA.sem, 2)
            phase_one(0, None, None)
            phase_two(None, 0)
            project(0, None)
            phase_one(1, 0, None)
            phase_two(0, 1)
            project(1, 0)
            with dve.Fori(2, G) as g:
                phase_one(g, g - 1, g - 2)
                phase_two(g - 1, g, BEGUN)
                project(g, g - 1)
            phase_one(None, G - 1, G - 2)
            phase_two(G - 1, None)
            phase_one(None, None, G - 1)

        @block.gpsimd
        def _(pool):
            Q = nc.gpsimd
            chain_a, chain_b = Chain(c_pool_a, pool), Chain(c_pool_b, pool)

            def scales(g, k, link):
                mv, sm = mvs[k > 0], sms[k > 0]

                def power(dst, src):
                    return Q.tensor_tensor(sm[:, dst, :], sm[:, src, :], half[:], ALU.pow)

                pool.wait_ge(s_mv[k].sem, s_mv[k].at(g))
                mean, var = mv[:, :, 0], mv[:, :, 1]
                if k == 1:
                    link(Q.tensor_tensor(sm[:, 0, :], mean, mean, ALU.mult))
                    link(Q.tensor_tensor(sm[:, 0, :], sm[:, 0, :], var, ALU.add))
                    hold(pool, "pool")
                    link(Q.tensor_scalar(sm[:, 1, :], sm[:, 0, :], 1e-6, None, ALU.add))
                    power(2, 1).then_inc(s_sc[k].sem, 1)
                    return
                hold(pool, "pool")
                link(Q.tensor_scalar(sm[:, 1, :], var, 1e-5, None, ALU.add))
                if k == 3:
                    power(2, 1).then_inc(s_sc[k].sem, 1)
                    return
                link(power(2, 1))
                link(Q.tensor_tensor(sm[:, 3, :], var, sm[:, 2, :], ALU.mult))
                link(Q.tensor_tensor(sm[:, 4, :], sm[:, 3, :], sm[:, 2, :], ALU.mult))
                hold(pool, "pool")
                link(Q.tensor_scalar(sm[:, 3, :], sm[:, 4, :], 1e-6 if k == 0 else 1e-5, None, ALU.add))
                link(power(5, 3))
                Q.tensor_tensor(sm[:, 6, :], sm[:, 2, :], sm[:, 5, :], ALU.mult).then_inc(s_sc[k].sem, 1)

            def broadcast(g, s):
                slot = s_row[s % NROW]
                pool.wait_ge(slot.sem, slot.at(g, 32 * (s // NROW + 1)))
                if s >= NBC:
                    pool.wait_ge(s_hc.sem, s_hc.at(g, MD * (s - NBC + 1)))
                    pool.wait_ge(s_add.sem, s_add.at(g, MD * (s - NBC + 1)))
                elif s == 0:
                    pool.wait_ge(s_rst.sem, s_rst.at(g))
                hold(pool, "pool")
                r = 32 * (s % NROW)
                Q.partition_broadcast(bc[:, s % NBC, :], brows[r:r + 1, :]).then_inc(s_bc.sem, 1)
                pool.wait_ge(s_bc.sem, s_bc.at(g, s + 1))

            def scan_step(g, kind, k):
                if kind == "dec" and k == 0:
                    pool.wait_ge(s_acc0.sem, s_acc0.at(g))
                    broadcast(g, 0)
                    broadcast(g, 1)
                elif kind == "scn" and k >= 2:
                    j = k - 2
                    state, m = divmod(j, MD)
                    pool.wait_ge(s_hc.sem, s_hc.at(g, j + 1))
                    if state:
                        pool.wait_ge(s_add.sem, s_add.at(g, j - MD + 1))
                    y = tok(acc[:, m, :])
                    Q.tensor_tensor(y, y, padded(ring[:, j % NRING, :]), ALU.add).then_inc(s_add.sem, 1)
                    if m == MD - 1 and state + NBC < S:
                        broadcast(g, state + NBC)

            def phase_one(a, b, e):
                if a is not None:
                    chain_a.begin(a)
                if b is not None:
                    chain_b.begin(b)
                for kind, k in first_phase(a is not None, b is not None, e is not None)[0]:
                    if kind == "norm":
                        scales(b if k else a, k, (chain_b if k else chain_a).link)
                    elif kind in ("dec", "scn"):
                        scan_step(a, kind, k)

            def phase_two(b, s, first_b, begun=(0, 0)):
                for kind, k in second_phase(b is not None, s is not None, *begun):
                    if kind in ("dec", "scn"):
                        scan_step(s, kind, k)
                    elif kind == "norm":
                        scales(b, k, chain_b.link)
                        if k == 3:
                            if not first_b:
                                pool.wait_ge(s_out.sem, s_out.at(b - 1))
                            for t, (t0, rows) in enumerate(TILES):
                                Q.tensor_tensor(acc2[0:rows, t, :], h0[0:rows, t, :], hn[0:rows, t, :], ALU.add
                                                ).then_inc(s_h1x.sem, 1)
                    elif kind == "tr" and k == 3:
                        for t, (t0, rows) in enumerate(TILES):
                            pool.wait_ge(e_ow.sem, e_ow.at(b, t + 1))
                            Q.tensor_tensor(hn[0:rows, t, :], xa[0:rows, t, :], mb2[0:rows, :], ALU.add
                                            ).then_inc(s_x5b.sem, 1)

            pool.wait_ge(s_setup.sem, SETUP)
            pool.wait_ge(s_negA.sem, 2)
            phase_one(0, None, None)
            phase_two(None, 0, True)
            phase_one(1, 0, None)
            phase_two(0, 1, True)
            with pool.Fori(2, G) as g:
                phase_one(g, g - 1, g - 2)
                phase_two(g - 1, g, False, BEGUN)
            phase_one(None, G - 1, G - 2)
            phase_two(G - 1, None, False)


def layouts(np, i):
    f = lambda a: np.ascontiguousarray(np.asarray(a, np.float32))

    def tiles(a, m=None):
        k = -(-a.shape[0] // 128)
        out = np.zeros((k * 128, a.shape[1]), np.float32)
        out[:a.shape[0]] = a
        return out.reshape(k, 128, -1).transpose(1, 0, 2)

    def cols(v, k):
        out = np.zeros(k * 128, np.float32)
        out[:v.size] = v.reshape(-1)
        return out.reshape(k, 128).T

    w = {n: np.asarray(v) for n, v in i.items()}
    A, F = "L0_attn_", "L0_ffn_"
    x = w["x"].reshape(B // 2, 2, C_IN, SIDE, PATCH, SIDE, PATCH).transpose(0, 2, 4, 6, 1, 3, 5)
    x = x.reshape(B // 2, KC, 128, 2 * NP).transpose(0, 2, 1, 3)
    pos = w["L0_tok_pos_table"].reshape(32, 32, E)[::32 // SIDE, ::32 // SIDE].reshape(NP, E)
    inw, inb = w[F + "in_w"], w[F + "in_b"]
    bias_row = lambda a, b: np.concatenate([a, b.reshape(1, -1)])
    wqk = bias_row(inw[:2 * E].T, inb[:2 * E])
    split = np.zeros((4, 32, 2, HP), np.float32)
    for kind, parts in enumerate(((0, 1), (2,), (0, 2), (1,))):
        for a in range(2):
            for part in parts:
                split[kind, HD * a:HD * a + HD, a, HD * part:HD * part + HD] = np.eye(HD)
    wo = np.zeros((H, VW, E), np.float32)
    wo[:, :HD] = w[F + "out_w"].T.reshape(H, HD, E)
    wo[0, HD] = w[F + "out_b"]
    pick = np.zeros((VW, VW), np.float32)
    pick[HD, :] = 1.0
    place = np.zeros((2, H, MH, 128), np.float32)
    for h in range(H):
        for part in range(2):
            place[part, h, h // 2, HP * (h % 2) + 3 * HD + part] = 1.0
    vecs = {"w1n": cols(w[A + "w_norm1"], 2), "wfn": cols(w[A + "w_ffn_norm"], 2),
            "g1": cols(w[F + "ln1_g"], 2), "b1": cols(w[F + "ln1_b"], 2),
            "g2": cols(w[F + "ln2_g"], 2), "b2": cols(w[F + "ln2_b"], 2),
            "bdt": cols(w[A + "b_dt"], MD), "dsk": cols(w[A + "D_skip"], MD),
            "alog": w[A + "A_log"].reshape(MD, 128, S).transpose(1, 0, 2).reshape(128, MD * S),
            "kone": (np.arange(128) % HP // 2 == 3 * HD // 2).reshape(128, 1),
            "mb1": cols(w[F + "mlp_b1"], MM),
            "eb1": w[F + "exp_b1"].reshape(NEXP * MM, 128).T}
    a = {"patches": x, "txt": w["txt"], "place": place.reshape(2 * H, MH, 128),
         "cw": tiles(w["L0_tok_conv_w"].reshape(E, -1).T),
         "win": tiles(w[A + "W_in"].T), "wgate": tiles(w[A + "W_gate"].T), "wxp": tiles(w[A + "W_xproj"].T),
         "wdt": tiles(w[A + "W_dt"].T), "wout": tiles(w[A + "W_out"].T), "wgf": tiles(w[A + "W_gate_ffn"].T),
         "wup": tiles(w[A + "W_up"].T), "wdn": tiles(w[A + "W_down"].T),
         "wqk": tiles(wqk), "split": np.tile(split.reshape(4, 32, 128).transpose(1, 0, 2), (4, 1, 1)),
         "wv": tiles(bias_row(inw[2 * E:].T, inb[2 * E:])),
         "wo": tiles(wo.reshape(H * VW, E)), "pick": np.kron(np.eye(128 // VW), pick),
         "mw1": tiles(w[F + "mlp_w1"]), "mw2": tiles(w[F + "mlp_w2"]),
         "gw": tiles(bias_row(w[F + "gate_w"].T, w[F + "gate_b"])),
         "ew": np.stack([np.concatenate([tiles(w[F + n][e]).reshape(128, -1) for n in ("exp_w1", "exp_w2")], 1)
                         for e in range(NEXP)]),
         "vec": np.concatenate([vecs[n] for n in VEC], 1),
         "pos": np.concatenate([pos, pos]), "cb": np.tile(w["L0_tok_conv_b"], (128, 1)),
         "mb2": np.tile(w[F + "mlp_b2"], (128, 1)), "eb2": w[F + "exp_b2"],
         "ident": np.eye(128), "earlier": np.tile(np.tril(np.ones((NEXP, NEXP)), -1), (128, 1, 1))}
    return {n: f(v) for n, v in a.items()}


def kernel(**inputs):
    import numpy as np
    import concourse.bacc as bacc
    from concourse.bass_utils import run_bass_kernel_spmd as run

    nc = bacc.Bacc("TRN2", target_bir_lowering=False, num_devices=1)
    arrays, dram = {}, {}
    for name, a in layouts(np, inputs).items():
        arrays["in_" + name] = a
        dram[name] = nc.dram_tensor("in_" + name, a.shape, F32, kind="ExternalInput").ap()
    out = nc.dram_tensor("out", (B, L, E), F32, kind="ExternalOutput").ap()
    early_fusion_program(nc, dram, out.rearrange("(g b) l e -> g (b l) e", b=GB))
    r = run(nc, [arrays], core_ids=[0])
    return r.results[0]["out"]
```
